# Optimizing a Trainium2 kernel written in Bass

```python
import numpy as np
import jax
import jax.numpy as jnp

def _softmax(x, axis=-1):
    return jax.nn.softmax(x, axis=axis)

def _gelu(x):
    return jax.nn.gelu(x, approximate=True)

def _silu(x):
    return jax.nn.silu(x)

def _sigmoid(x):
    return jax.nn.sigmoid(x)

def _layernorm(x, axis=-1, eps=1e-05):
    m = jnp.mean(x, axis=axis, keepdims=True)
    v = jnp.var(x, axis=axis, keepdims=True)
    return (x - m) / jnp.sqrt(v + eps)

def _scatter_add(tgt, idx, src, axis=0):
    return tgt.at[idx].add(src)

def _segment_sum(src, seg, n):
    return jax.ops.segment_sum(src, seg, n)
kernel_name = 'mk_sandwich_d1_jaxref_r4_d238b4'

def setup_inputs(seed: int=0):
    np.random.seed(seed)
    _w = jnp.asarray

    def _L0_attn_setup():
        import jax, jax.numpy as jnp
        import numpy as np
        from jax import lax
        D_MODEL = 256
        KERNEL = 7
        RMS_EPS = 1.1920929e-07

        def _depthwise_conv1d(x_bds, w, b):
            D = x_bds.shape[1]
            pad = w.shape[-1] // 2
            y = lax.conv_general_dilated(x_bds, w, window_strides=(1,), padding=[(pad, pad)], feature_group_count=D, dimension_numbers=('NCH', 'OIH', 'NCH'))
            return y + b[None, :, None]

        def _decay_scan(gated, decay):
            a = jnp.broadcast_to(decay[None, :, None], gated.shape)

            def combine(c1, c2):
                a1, b1 = c1
                a2, b2 = c2
                return (a1 * a2, a2 * b1 + b2)
            _, h = lax.associative_scan(combine, (a, gated), axis=2)
            return h
        key = jax.random.key(seed)
        ks = jax.random.split(key, 6)
        B, S, D, K = (4, 1024, D_MODEL, KERNEL)
        x = jax.random.normal(ks[0], (B, S, D), dtype=jnp.float32)
        gate_w = jax.random.normal(ks[1], (D, 1, K), dtype=jnp.float32) * 0.1
        gate_b = jnp.zeros((D,), dtype=jnp.float32)
        cand_w = jax.random.normal(ks[2], (D, 1, K), dtype=jnp.float32) * 0.1
        cand_b = jnp.zeros((D,), dtype=jnp.float32)
        log_decay = jnp.full((D,), np.log(0.1), dtype=jnp.float32)
        out_w = jax.random.normal(ks[3], (D, D), dtype=jnp.float32) * 0.02
        out_b = jnp.zeros((D,), dtype=jnp.float32)
        norm_w = jnp.ones((D,), dtype=jnp.float32)
        return {'x': x, 'gate_w': gate_w, 'gate_b': gate_b, 'cand_w': cand_w, 'cand_b': cand_b, 'log_decay': log_decay, 'out_w': out_w, 'out_b': out_b, 'norm_w': norm_w}
    _L0_attn_in = _L0_attn_setup()

    def _L0_ffn_setup():
        import jax, jax.numpy as jnp
        import numpy as np
        B, S, D, H, E, K, F = (1, 256, 256, 16, 8, 2, 1024)

        def layernorm(x, g, b, eps=1e-05):
            m = x.mean(-1, keepdims=True)
            v = ((x - m) ** 2).mean(-1, keepdims=True)
            return (x - m) * jax.lax.rsqrt(v + eps) * g + b
        key = jax.random.key(seed)
        ks = jax.random.split(key, 8)
        n = lambda k, shape, sc: jax.random.normal(k, shape, dtype=jnp.float32) * sc
        return {'x': n(ks[0], (B, S, D), 1.0), 'w_qkv': n(ks[1], (D, 3 * D), D ** (-0.5)), 'w_o': n(ks[2], (D, D), D ** (-0.5)), 'g1': jnp.ones((D,), jnp.float32), 'b1': jnp.zeros((D,), jnp.float32), 'wg': n(ks[3], (D, E), D ** (-0.5)), 'w1': n(ks[4], (E, D, F), D ** (-0.5)), 'bb1': jnp.zeros((E, F), jnp.float32), 'w2': n(ks[5], (E, F, D), F ** (-0.5)), 'bb2': jnp.zeros((E, D), jnp.float32), 'g2': jnp.ones((D,), jnp.float32), 'b2': jnp.zeros((D,), jnp.float32)}
    _L0_ffn_in = _L0_ffn_setup()
    _d = {'L0_attn_x': _L0_attn_in['x'], 'L0_attn_gate_w': _L0_attn_in['gate_w'], 'L0_attn_gate_b': _L0_attn_in['gate_b'], 'L0_attn_cand_w': _L0_attn_in['cand_w'], 'L0_attn_cand_b': _L0_attn_in['cand_b'], 'L0_attn_log_decay': _L0_attn_in['log_decay'], 'L0_attn_out_w': _L0_attn_in['out_w'], 'L0_attn_out_b': _L0_attn_in['out_b'], 'L0_attn_norm_w': _L0_attn_in['norm_w'], 'L0_ffn_w_qkv': _L0_ffn_in['w_qkv'], 'L0_ffn_w_o': _L0_ffn_in['w_o'], 'L0_ffn_g1': _L0_ffn_in['g1'], 'L0_ffn_b1': _L0_ffn_in['b1'], 'L0_ffn_wg': _L0_ffn_in['wg'], 'L0_ffn_w1': _L0_ffn_in['w1'], 'L0_ffn_bb1': _L0_ffn_in['bb1'], 'L0_ffn_w2': _L0_ffn_in['w2'], 'L0_ffn_bb2': _L0_ffn_in['bb2'], 'L0_ffn_g2': _L0_ffn_in['g2'], 'L0_ffn_b2': _L0_ffn_in['b2']}
    _x0 = _d['L0_attn_x']
    _d['L0_attn_x'] = jax.random.normal(jax.random.fold_in(jax.random.key(seed), 1), (1, 4096, 256), dtype=_x0.dtype)
    del _x0
    return _d

def reference(L0_attn_x, L0_attn_gate_w, L0_attn_gate_b, L0_attn_cand_w, L0_attn_cand_b, L0_attn_log_decay, L0_attn_out_w, L0_attn_out_b, L0_attn_norm_w, L0_ffn_w_qkv, L0_ffn_w_o, L0_ffn_g1, L0_ffn_b1, L0_ffn_wg, L0_ffn_w1, L0_ffn_bb1, L0_ffn_w2, L0_ffn_bb2, L0_ffn_g2, L0_ffn_b2):

    def _L0_attn_ref(x, gate_w, gate_b, cand_w, cand_b, log_decay, out_w, out_b, norm_w):
        import jax, jax.numpy as jnp
        import numpy as np
        from jax import lax
        D_MODEL = 256
        KERNEL = 7
        RMS_EPS = 1.1920929e-07

        def _depthwise_conv1d(x_bds, w, b):
            D = x_bds.shape[1]
            pad = w.shape[-1] // 2
            y = lax.conv_general_dilated(x_bds, w, window_strides=(1,), padding=[(pad, pad)], feature_group_count=D, dimension_numbers=('NCH', 'OIH', 'NCH'))
            return y + b[None, :, None]

        def _decay_scan(gated, decay):
            a = jnp.broadcast_to(decay[None, :, None], gated.shape)

            def combine(c1, c2):
                a1, b1 = c1
                a2, b2 = c2
                return (a1 * a2, a2 * b1 + b2)
            _, h = lax.associative_scan(combine, (a, gated), axis=2)
            return h
        residual = x
        x_t = jnp.transpose(x, (0, 2, 1))
        gate = jax.nn.sigmoid(_depthwise_conv1d(x_t, gate_w, gate_b))
        cand = jnp.tanh(_depthwise_conv1d(x_t, cand_w, cand_b))
        gated = gate * cand
        decay = jnp.exp(log_decay)
        h = _decay_scan(gated, decay)
        h = jnp.transpose(h, (0, 2, 1))
        out = jnp.einsum('bsd,ed->bse', h, out_w) + out_b
        y = out + residual
        ms = jnp.mean(y * y, axis=-1, keepdims=True)
        return y * lax.rsqrt(ms + RMS_EPS) * norm_w

    def _L0_ffn_ref(x, w_qkv, w_o, g1, b1, wg, w1, bb1, w2, bb2, g2, b2):
        import jax, jax.numpy as jnp
        import numpy as np
        B, S, D, H, E, K, F = (1, 256, 256, 16, 8, 2, 1024)

        def layernorm(x, g, b, eps=1e-05):
            m = x.mean(-1, keepdims=True)
            v = ((x - m) ** 2).mean(-1, keepdims=True)
            return (x - m) * jax.lax.rsqrt(v + eps) * g + b
        b, s, d = x.shape
        hd = d // H
        qkv = x @ w_qkv
        q, k, v = jnp.split(qkv, 3, axis=-1)
        to_heads = lambda t: t.reshape(b, s, H, hd).transpose(0, 2, 1, 3)
        q, k, v = (to_heads(q), to_heads(k), to_heads(v))
        scores = jnp.einsum('bhqd,bhkd->bhqk', q, k) / jnp.sqrt(jnp.float32(hd))
        causal = jnp.tril(jnp.ones((s, s), bool))
        scores = jnp.where(causal, scores, jnp.finfo(scores.dtype).min)
        attn = jax.nn.softmax(scores, axis=-1)
        o = jnp.einsum('bhqk,bhkd->bhqd', attn, v)
        o = o.transpose(0, 2, 1, 3).reshape(b, s, d) @ w_o
        h = layernorm(x + o, g1, b1)
        probs = jax.nn.softmax(h @ wg, axis=-1)
        topv, topi = jax.lax.top_k(probs, K)
        topv = topv / topv.sum(-1, keepdims=True)
        w = (topv[..., None] * jax.nn.one_hot(topi, E, dtype=h.dtype)).sum(-2)
        h1 = jax.nn.gelu(jnp.einsum('bsd,edf->ebsf', h, w1) + bb1[:, None, None, :])
        y = jnp.einsum('ebsf,efd->ebsd', h1, w2) + bb2[:, None, None, :]
        moe = jnp.einsum('ebsd,bse->bsd', y, w)
        return layernorm(h + moe, g2, b2)
    x = L0_attn_x
    x = x + _layernorm(_L0_attn_ref(_layernorm(x, axis=-1), L0_attn_gate_w, L0_attn_gate_b, L0_attn_cand_w, L0_attn_cand_b, L0_attn_log_decay, L0_attn_out_w, L0_attn_out_b, L0_attn_norm_w), axis=-1)
    x = x + _layernorm(_L0_ffn_ref(_layernorm(x, axis=-1), L0_ffn_w_qkv, L0_ffn_w_o, L0_ffn_g1, L0_ffn_b1, L0_ffn_wg, L0_ffn_w1, L0_ffn_bb1, L0_ffn_w2, L0_ffn_bb2, L0_ffn_g2, L0_ffn_b2), axis=-1)
    return x

_drawn_inputs = setup_inputs


def setup_inputs(seed=0):
    import zlib

    import numpy as np

    out = dict(_drawn_inputs(seed))
    spreads = {'L0_attn_gate_b': (0.0, 0.8),
     'L0_attn_cand_b': (0.0, 0.484),
     'L0_attn_log_decay': (-2.3025851249694824, 0.6),
     'L0_attn_out_b': (0.0, 0.1),
     'L0_attn_norm_w': (1.0, 0.2),
     'L0_ffn_g1': (1.0, 0.2),
     'L0_ffn_b1': (0.0, 0.1),
     'L0_ffn_bb1': (0.0, 0.528),
     'L0_ffn_bb2': (0.0, 0.37),
     'L0_ffn_g2': (1.0, 0.2),
     'L0_ffn_b2': (0.0, 0.1)}
    factors = {'L0_attn_gate_w': 8.0}
    for name, (base, spread) in spreads.items():
        noise = np.random.default_rng([zlib.crc32(name.encode()), seed]).standard_normal(out[name].shape)
        drawn = base * np.exp(spread * noise) if base else spread * noise
        out[name] = jnp.asarray(drawn.astype(out[name].dtype))
    for name, factor in factors.items():
        out[name] = (out[name] * factor).astype(out[name].dtype)
    return out
```

```python
from contextlib import ExitStack

import concourse.bass as bass
from concourse import mybir

ALU = mybir.AluOpType
ACT = mybir.ActivationFunctionType
AX = mybir.AxisListType
F32 = mybir.dt.float32
F16 = mybir.dt.float16
BF16 = mybir.dt.bfloat16
U32 = mybir.dt.uint32
I32 = mybir.dt.int32

P = 128
S = 4096
D = 256
DH = D // P
TILES = S // P
CHUNK = 512
CHUNKS = S // CHUNK
TPC = CHUNK // P
TAPS = 7
PAD = TAPS // 2
HEADS = 16
HD = D // HEADS
GROUP = 4
GROUPS = HEADS // GROUP
EXPERTS = 8
F = 1024
FB = F // P
LN_EPS = 1e-5
RMS_EPS = 1.1920929e-07
MASKED = -1e30
ds = bass.ds


def ge(eng, sem, value):
    if not isinstance(value, int) or value > 0:
        eng.wait_ge(sem, value)


def pause(eng, sem, value, passed):
    eng.wait_ge(sem, value)
    eng.sem_inc(passed, 1)


class Memory:

    def __init__(self, nc, ctx, tag):
        self.nc, self.ctx, self.tag, self.sems = nc, ctx, tag, []

    def sb(self, name, shape, dt=F32):
        return self.ctx.enter_context(self.nc.sbuf_tensor(f"{self.tag}_{name}", shape, dt))

    def ps(self, name, shape=(P, CHUNK), dt=F32):
        return self.ctx.enter_context(self.nc.psum_tensor(f"{self.tag}_{name}", list(shape), dt))

    def sem(self, name):
        self.sems.append(self.ctx.enter_context(self.nc.semaphore(f"{self.tag}_{name}")))
        return self.sems[-1]

    def clear(self):
        with self.nc.Block() as block:
            @block.gpsimd
            def _(pool):
                for s in self.sems:
                    pool.sem_clear(s)


def front_phase(nc, ident, x_in, gate_w, gate_b, cand_w, cand_b, log_decay, out_wT, out_b, norm_w, w_qkv,
                x1_d, u2_d, qk_d, v_d):
    with ExitStack() as ctx:
        m = Memory(nc, ctx, "f")
        X = m.sb("X", [P, TILES, D])
        UB = m.sb("UB", [P, TILES, D])
        uT = m.sb("uT", [P, DH, S + 2 * PAD])
        stats = m.sb("stats", [P, TILES, 6])
        mean = m.sb("mean", [P, TILES])
        rstd = m.sb("rstd", [P, TILES])
        tmp = m.sb("tmp", [P, 4, TILES])
        us = m.sb("us", [P, 2, TPC, D])
        taps = m.sb("taps", [P, 2, DH, TAPS])
        bias = m.sb("bias", [P, 2, DH])
        decay = m.sb("decay", [P, 2, DH])
        diag = m.sb("diag", [P, DH, TAPS, P])
        wout = m.sb("wout", [P, DH, D])
        wqkv = m.sb("wqkv", [P, DH, 3 * D])
        rows = m.sb("rows", [P, 2, D])
        tanh_g = m.sb("tanh_g", [P, 2, DH, CHUNK])
        cand = m.sb("cand", [P, DH, CHUNK])
        tanh_c = m.sb("tanh_c", [P, 2, DH, CHUNK])
        gated = m.sb("gated", [P, DH, CHUNK])
        hT = m.sb("hT", [P, 2, DH, CHUNK])
        y = m.sb("y", [P, TPC, D])
        junk = m.sb("junk", [P, D])
        ssq = m.sb("ssq", [P, TPC])
        z = m.sb("z", [P, TPC, D])
        r = m.sb("r", [P, TPC, D])
        x1 = m.sb("x1", [P, TPC, D])
        u2 = m.sb("u2", [P, TPC, D])
        st = m.sb("st", [P, 2, TPC, 6])
        mv = m.sb("mv", [P, 2, TPC, 2])
        sm = m.sb("sm", [P, 8, TPC])
        u2T = m.sb("u2T", [P, DH, CHUNK])
        rest = m.sb("rest", [P, 4, CHUNK])
        parts = m.sb("parts", [P, 3, 4, CHUNK], BF16)
        vt = m.sb("vt", [P, GROUPS, TPC, GROUP, HD + 1])
        G = [m.ps(f"G{h}") for h in range(DH)]
        Y = [m.ps(f"Y{h}") for h in range(2)]
        T = [m.ps(f"T{h}") for h in range(DH)]
        Q = [m.ps(f"Q{h}") for h in range(2)]

        s = {n: m.sem(n) for n in (
            "passed x_even x_odd consts ident0 ident1 exp_done diag_done ones stats1 mom var1 sd1 rstd1 us_done tr1 "
            "ut_done ub_done gate_conv tap tanh_g tanh_c gated scan proj y ssq z stz mvz a1 sdz a2 r x1 stx mvx "
            "a3 sdx a4 u2 tr2 u2T qk v hi res mid low vt x1_st u2_st qk_st v_st").split()}
        x_loaded = (s["x_even"], s["x_odd"])
        body = ctx.enter_context(ExitStack())
        block = body.enter_context(nc.Block())
        consts = [(taps[:, 0], gate_w.rearrange("(h p) o k -> p h (o k)", p=P)),
                  (taps[:, 1], cand_w.rearrange("(h p) o k -> p h (o k)", p=P)),
                  (bias[:, 0], gate_b),
                  (bias[:, 1], cand_b),
                  (decay[:, 0], log_decay),
                  (wout[:, :, :], out_wT.rearrange("(h p) e -> p h e", p=P)),
                  (wqkv[:, :, :], w_qkv.rearrange("(h p) e -> p h e", p=P)),
                  (rows[:, 0], out_b.partition_broadcast(P)),
                  (rows[:, 1], norm_w.partition_broadcast(P))]
        CONSTS = 16 * len(consts)

        def nothing(c, i, b):
            pass

        def stages(fori, stage1, stage2, stage3, stage2b=nothing):
            def pair(i):
                for b in range(2):
                    stage1(2 * i + (2 + b), i + 1, b)
                    stage2(2 * i + (1 + b), i + b, 1 - b)
                    stage3(2 * i + b, i, b)
                    stage2b(2 * i + (1 + b), i + b, 1 - b)

            stage1(0, 0, 0)
            stage1(1, 0, 1)
            stage2(0, 0, 0)
            stage2b(0, 0, 0)
            pair(0)
            with fori(1, (CHUNKS - 2) // 2) as i:
                pair(i)
            stage2(CHUNKS - 1, CHUNKS // 2 - 1, 1)
            stage3(CHUNKS - 2, CHUNKS // 2 - 1, 0)
            stage2b(CHUNKS - 1, CHUNKS // 2 - 1, 1)
            stage3(CHUNKS - 1, CHUNKS // 2 - 1, 1)

        @block.sync
        def _(sp):
            xv = x_in.rearrange("(c t p) d -> c p t d", p=P, t=TPC)
            for c in range(CHUNKS):
                ge(sp, x_loaded[c % 2], 16 * (c // 2))
                sp.dma_start(X[:, c * TPC:(c + 1) * TPC, :], xv[c]).then_inc(x_loaded[c % 2], 16)

            def stage2(c, i, b):
                sp.wait_ge(s["x1"], c + 1)
                sp.dma_start(x1_d.rearrange("(t p) d -> p t d", p=P)[:, ds(c * TPC, TPC), :], x1[:, :, :])\
                  .then_inc(s["x1_st"], 16)
                sp.wait_ge(s["u2"], c * TPC + TPC)
                sp.dma_start(u2_d.rearrange("(t p) d -> p t d", p=P)[:, ds(c * TPC, TPC), :], u2[:, :, :])\
                  .then_inc(s["u2_st"], 16)

            def stage3(c, i, b):
                sp.wait_ge(s["vt"], c * TPC + (TPC + 1))
                sp.dma_start(v_d.rearrange("g p t h d -> p g t (h d)")[:, :, ds(c * TPC, TPC), :],
                             vt[:, :, :, :, :].rearrange("p g t h d -> p g t (h d)")).then_inc(s["v_st"], 16)
                sp.wait_ge(s["hi"], 4 * c + 4)
                sp.wait_ge(s["mid"], 4 * c + 4)
                sp.wait_ge(s["low"], 4 * c + 4)
                sp.dma_start(qk_d.rearrange("s q p n -> p (s q) n")[:, :, ds(c * CHUNK, CHUNK)],
                             parts[:, :, :, :].rearrange("p s q n -> p (s q) n")).then_inc(s["qk_st"], 16)

            stages(sp.Fori, nothing, stage2, stage3)
            for n in ("x1_st", "u2_st", "v_st", "qk_st"):
                sp.wait_ge(s[n], 16 * CHUNKS)

        @block.gpsimd
        def _(pool):
            pool.memset(ident[:, :], 0.0).then_inc(s["ident0"], 1)
            for dst, src in consts:
                pool.dma_start(dst, src).then_inc(s["consts"], 16)
            pool.wait_ge(s["ident0"], 1)
            pool.affine_select(out=ident[:, :], in_=ident[:, :], compare_op=ALU.not_equal, fill=1.0, base=0,
                               pattern=[[-1, P]], channel_multiplier=1).then_inc(s["ident1"], 1)
            pool.memset(vt[:, :, :, :, HD:HD + 1], 1.0).then_inc(s["vt"], 1)
            pool.wait_ge(s["consts"], CONSTS)
            with pool.Fori(0, CHUNKS // 2) as i:
                for b in range(2):
                    pool.wait_ge(s["us_done"], (2 * i + b) * TPC + TPC)
                    pool.tensor_tensor(UB[:, ds((2 * i + b) * TPC, TPC), :], us[:, b],
                                       rows[:, 0].unsqueeze(1).broadcast_to([P, TPC, D]), ALU.add)\
                        .then_inc(s["ub_done"], 1)

            def stage2(c, i, b):
                pool.wait_ge(s["y"], 2 * c + 2)
                ge(pool, s["r"], TPC * c)
                pool.tensor_tensor(z[:, :, :], y[:, :, :], rows[:, 1].unsqueeze(1).broadcast_to([P, TPC, D]),
                                   ALU.mult).then_inc(s["z"], 1)
                pool.wait_ge(s["r"], TPC * c + TPC)
                ge(pool, s["x1_st"], 16 * c)
                ge(pool, s["u2"], TPC * c)
                pool.tensor_tensor(x1[:, :, :], r[:, :, :], X[:, ds(c * TPC, TPC), :], ALU.add)\
                    .then_inc(s["x1"], 1)

            def stage3(c, i, b):
                ge(pool, s["qk_st"], 16 * c)
                for q in range(4):
                    pool.wait_ge(s["mid"], 4 * c + q + 1)
                    pool.tensor_tensor(parts[:, 2, q, :], rest[:, q, :], parts[:, 1, q, :], ALU.subtract)\
                        .then_inc(s["low"], 1)

            stages(pool.Fori, nothing, stage2, stage3)

        @block.scalar
        def _(act):
            act.wait_ge(s["consts"], CONSTS)
            act.activation(decay[:, 1], decay[:, 0], ACT.Exp).then_inc(s["exp_done"], 1)
            act.wait_ge(s["var1"], 1)
            act.activation(tmp[:, 3, :], tmp[:, 2, :], ACT.Sqrt).then_inc(s["sd1"], 1)
            act.mul(bias[:, 0], bias[:, 0], 0.5).then_inc(s["exp_done"], 1)
            with act.Fori(0, CHUNKS) as c:
                for h in range(DH):
                    act.wait_ge(s["tr1"], c * DH + (h + 1))
                    act.copy(uT[:, h, ds(c * CHUNK + PAD, CHUNK)], T[h][:, :]).then_inc(s["ut_done"], 1)
            act.wait_ge(s["exp_done"], 2)

            def stage1(c, i, b):
                for h in range(DH):
                    act.wait_ge(s["gate_conv"], c * DH + (h + 1))
                    ge(act, s["gated"], DH * (c - 1))
                    act.activation(tanh_g[:, b, h], G[h][:, :], ACT.Tanh, bias=bias[:, 0, h:h + 1], scale=0.5)\
                       .then_inc(s["tanh_g"], 1)
                for h in range(DH):
                    act.wait_ge(s["tap"], (c + 1) * DH * TAPS)
                    act.activation(tanh_c[:, b, h], cand[:, h], ACT.Tanh, bias=bias[:, 1, h:h + 1])\
                       .then_inc(s["tanh_c"], 1)

            def stage2(c, i, b):
                act.wait_ge(s["y"], 2 * c + 2)
                for t in range(TPC):
                    if t:
                        act.wait_ge(s["ssq"], TPC * c + t)
                    else:
                        ge(act, s["ssq"], TPC * c)
                    act.activation(junk[:, :], y[:, t], ACT.Square, accum_out=ssq[:, t:t + 1])\
                       .then_inc(s["ssq"], 1)
                act.wait_ge(s["a1"], 2 * c + 2)
                act.activation(sm[:, 2, :], sm[:, 1, :], ACT.Sqrt).then_inc(s["sdz"], 1)
                act.wait_ge(s["a2"], 2 * c + 2)
                ge(act, s["x1"], c)
                for t in range(TPC):
                    act.activation(r[:, t], z[:, t], ACT.Identity, bias=sm[:, 4, t:t + 1],
                                   scale=sm[:, 3, t:t + 1]).then_inc(s["r"], 1)
                act.wait_ge(s["a3"], c + 1)
                act.activation(sm[:, 6, :], sm[:, 5, :], ACT.Sqrt).then_inc(s["sdx"], 1)

            def stage2b(c, i, b):
                for h in range(DH):
                    act.wait_ge(s["tr2"], c * DH + (h + 1))
                    ge(act, s["v"], TPC * c)
                    act.copy(u2T[:, h], T[h][:, :]).then_inc(s["u2T"], 1)

            def stage3(c, i, b):
                ge(act, s["qk_st"], 16 * c)
                for q in range(4):
                    act.wait_ge(s["qk"], 4 * c + q + 1)
                    act.copy(parts[:, 0, q], Q[q % 2][:, :]).then_inc(s["hi"], 1)
                    act.wait_ge(s["res"], 4 * c + q + 1)
                    act.copy(parts[:, 1, q], rest[:, q]).then_inc(s["mid"], 1)
                ge(act, s["v_st"], 16 * c)
                for t in range(TPC):
                    act.wait_ge(s["v"], TPC * c + t + 1)
                    act.copy(vt[:, :, t, :, 0:HD], Q[t % 2][:, 0:D].rearrange("p (g h d) -> p g h d", g=GROUPS, h=GROUP))\
                       .then_inc(s["vt"], 1)

            stages(act.Fori, stage1, stage2, stage3, stage2b)

        @block.vector
        def _(dve):
            dve.memset(uT[:, :, 0:PAD], 0.0).then_inc(s["ones"], 1)
            dve.memset(uT[:, :, S + PAD:S + 2 * PAD], 0.0).then_inc(s["ones"], 1)
            dve.memset(hT[:, 1, :, CHUNK - 1:CHUNK], 0.0).then_inc(s["ones"], 1)
            with dve.Fori(0, CHUNKS // 2) as i:
                for b in range(2):
                    dve.wait_ge(x_loaded[b], 16 * i + 16)
                    for t in range(TPC):
                        dve.bn_stats(stats[:, ds((2 * i + b) * TPC + t, 1), :].rearrange("p a b -> p (a b)"),
                                     X[:, ds((2 * i + b) * TPC + t, 1), :].rearrange("p a b -> p (a b)"))\
                           .then_inc(s["stats1"], 1)
            dve.wait_ge(s["stats1"], TILES)
            me, mo = stats[:, :, 1], stats[:, :, 4]
            dve.tensor_tensor(tmp[:, 0], me, mo, ALU.add).then_inc(s["mom"], 1)
            dve.tensor_tensor(tmp[:, 1], me, mo, ALU.subtract).then_inc(s["mom"], 1)
            dve.tensor_tensor(tmp[:, 2], stats[:, :, 2], stats[:, :, 5], ALU.add).then_inc(s["mom"], 1)
            dve.wait_ge(s["mom"], 3)
            dve.tensor_scalar(mean[:, :], tmp[:, 0], 0.5, None, ALU.mult).then_inc(s["mom"], 1)
            dve.tensor_scalar(tmp[:, 2], tmp[:, 2], 1.0 / D, LN_EPS, ALU.mult, ALU.add).then_inc(s["mom"], 1)
            dve.scalar_tensor_tensor(tmp[:, 1], tmp[:, 1], 0.25, tmp[:, 1], ALU.mult, ALU.mult).then_inc(s["mom"], 1)
            dve.wait_ge(s["mom"], 6)
            dve.tensor_tensor(tmp[:, 2], tmp[:, 2], tmp[:, 1], ALU.add).then_inc(s["var1"], 1)
            dve.wait_ge(s["sd1"], 1)
            dve.reciprocal(rstd[:, :], tmp[:, 3, :]).then_inc(s["rstd1"], 1)
            dve.wait_ge(s["rstd1"], 1)

            def apply(c, i, b):
                for t in range(TPC):
                    if not isinstance(i, int):
                        dve.wait_ge(s["tr1"], DH * (c - 1))
                        dve.wait_ge(s["ub_done"], c - 1)
                    n = c * TPC + t
                    dve.tensor_scalar(us[:, b, t], X[:, ds(n, 1), :].rearrange("p a b -> p (a b)"),
                                      mean[:, ds(n, 1)], rstd[:, ds(n, 1)], ALU.subtract, ALU.mult)\
                       .then_inc(s["us_done"], 1)
            apply(0, 0, 0)
            apply(1, 0, 1)
            with dve.Fori(0, (CHUNKS - 2) // 2) as i:
                for b in range(2):
                    apply(2 * i + (2 + b), i + 1, b)
            dve.wait_ge(s["consts"], CONSTS)
            dve.wait_ge(s["ident1"], 1)
            for h in range(DH):
                for k in range(TAPS):
                    dve.tensor_scalar(diag[:, h, k], ident[:, :], taps[:, 0, h, k:k + 1], None, ALU.mult)\
                       .then_inc(s["diag_done"], 1)
            dve.wait_ge(s["ut_done"], DH * CHUNKS)
            dve.wait_ge(s["ones"], 3)
            dve.wait_ge(s["exp_done"], 2)

            def conv(c, ks):
                for k in ks:
                    for h in range(DH):
                        n = k * DH + h
                        if k == 0:
                            ge(dve, s["tanh_c"], DH * c)
                            dve.tensor_scalar(cand[:, h], uT[:, h, ds(c * CHUNK, CHUNK)], taps[:, 1, h, 0:1],
                                              None, ALU.mult).then_inc(s["tap"], 1)
                        else:
                            dve.wait_ge(s["tap"], c * DH * TAPS + (n - DH + 1))
                            dve.scalar_tensor_tensor(cand[:, h], uT[:, h, ds(c * CHUNK + k, CHUNK)],
                                                     taps[:, 1, h, k:k + 1], cand[:, h], ALU.mult, ALU.add)\
                               .then_inc(s["tap"], 1)

            def stage1(c, i, b):
                conv(c, range(TAPS))
                for h in range(DH):
                    dve.wait_ge(s["tanh_g"], DH * c + (h + 1))
                    dve.wait_ge(s["tanh_c"], DH * c + (h + 1))
                    ge(dve, s["scan"], DH * (c - 1) + (h + 1))
                    dve.scalar_tensor_tensor(gated[:, h], tanh_g[:, b, h], 1.0, tanh_c[:, b, h], ALU.add, ALU.mult)\
                       .then_inc(s["gated"], 1)
                for h in range(DH):
                    dve.wait_ge(s["gated"], DH * c + (h + 1))
                    if h == 0:
                        ge(dve, s["proj"], 2 * (c - 1))
                    dve.tensor_tensor_scan(out=hT[:, b, h], data0=decay[:, 1, h:h + 1].broadcast_to([P, CHUNK]),
                                           data1=gated[:, h], initial=hT[:, 1 - b, h, CHUNK - 1:CHUNK],
                                           op0=ALU.mult, op1=ALU.add).then_inc(s["scan"], 1)

            def stage2(c, i, b):
                for j in range(2):
                    dve.wait_ge(s["proj"], 2 * c + j + 1)
                    ge(dve, s["z"], c)
                    ge(dve, s["ssq"], TPC * c)
                    dve.scalar_tensor_tensor(y[:, 2 * j:2 * j + 2].rearrange("p t d -> p (t d)"), Y[j][:, :], 0.5,
                                             UB[:, ds(c * TPC + 2 * j, 2), :].rearrange("p t d -> p (t d)"),
                                             ALU.mult, ALU.add).then_inc(s["y"], 1)
                dve.wait_ge(s["z"], c + 1)
                for t in range(TPC):
                    dve.bn_stats(st[:, 0, t], z[:, t]).then_inc(s["stz"], 1)
                pause(dve, s["stz"], TPC * c + TPC, s["passed"])
                for t in range(TPC):
                    dve.bn_aggr(mv[:, 0, t], st[:, 0, t]).then_inc(s["mvz"], 1)
                dve.wait_ge(s["ssq"], TPC * c + TPC)
                dve.tensor_scalar(sm[:, 0], ssq[:, :], LN_EPS / D, LN_EPS * RMS_EPS, ALU.mult, ALU.add)\
                   .then_inc(s["a1"], 1)
                dve.wait_ge(s["a1"], 2 * c + 1)
                dve.wait_ge(s["mvz"], TPC * c + TPC)
                dve.tensor_tensor(sm[:, 1], sm[:, 0], mv[:, 0, :, 1], ALU.add).then_inc(s["a1"], 1)
                dve.wait_ge(s["sdz"], c + 1)
                dve.reciprocal(sm[:, 3], sm[:, 2]).then_inc(s["a2"], 1)
                dve.wait_ge(s["a2"], 2 * c + 1)
                dve.scalar_tensor_tensor(sm[:, 4], mv[:, 0, :, 0], -1.0, sm[:, 3], ALU.mult, ALU.mult)\
                   .then_inc(s["a2"], 1)
                dve.wait_ge(s["x1"], c + 1)
                for t in range(TPC):
                    dve.bn_stats(st[:, 1, t], x1[:, t]).then_inc(s["stx"], 1)
                pause(dve, s["stx"], TPC * c + TPC, s["passed"])
                for t in range(TPC):
                    dve.bn_aggr(mv[:, 1, t], st[:, 1, t]).then_inc(s["mvx"], 1)
                dve.wait_ge(s["mvx"], TPC * c + TPC)
                dve.tensor_scalar(sm[:, 5], mv[:, 1, :, 1], LN_EPS, None, ALU.add).then_inc(s["a3"], 1)
                dve.wait_ge(s["sdx"], c + 1)
                dve.reciprocal(sm[:, 7], sm[:, 6]).then_inc(s["a4"], 1)
                dve.wait_ge(s["a4"], c + 1)
                ge(dve, s["u2_st"], 16 * c)
                ge(dve, s["tr2"], DH * c)
                for t in range(TPC):
                    dve.tensor_scalar(u2[:, t], x1[:, t], mv[:, 1, t, 0:1], sm[:, 7, t:t + 1],
                                      ALU.subtract, ALU.mult).then_inc(s["u2"], 1)

            def stage3(c, i, b):
                for q in range(4):
                    dve.wait_ge(s["hi"], 4 * c + q + 1)
                    ge(dve, s["low"], 4 * (c - 1) + q + 1)
                    dve.tensor_tensor(rest[:, q], Q[q % 2][:, :], parts[:, 0, q], ALU.subtract)\
                       .then_inc(s["res"], 1)

            stages(dve.Fori, stage1, stage2, stage3)

        @block.tensor
        def _(pe):
            pe.wait_ge(s["ident1"], 1)

            def transposes(c, src, waits):
                for h in range(DH):
                    for t in range(TPC):
                        pe.wait_ge(waits, c * TPC + t + 1)
                        mm = pe.transpose(T[h][:, t * P:(t + 1) * P], src(t, h), ident[:, :])
                    yield mm

            def transpose1(c, i, b):
                ge(pe, s["ut_done"], DH * c)
                for mm in transposes(c, lambda t, h: us[:, b, t, h * P:(h + 1) * P], s["us_done"]):
                    mm.then_inc(s["tr1"], 1)
            transpose1(0, 0, 0)
            transpose1(1, 0, 1)
            with pe.Fori(0, (CHUNKS - 2) // 2) as i:
                for b in range(2):
                    transpose1(2 * i + (2 + b), i + 1, b)
            pe.wait_ge(s["diag_done"], DH * TAPS)
            pe.wait_ge(s["ut_done"], DH * CHUNKS)
            pe.wait_ge(s["ones"], 3)
            pe.wait_ge(s["consts"], CONSTS)

            def stage1(c, i, b):
                for h in range(DH):
                    ge(pe, s["tanh_g"], DH * (c - 1) + (h + 1))
                    for k in range(TAPS):
                        mm = pe.matmul(G[h][:, :], diag[:, h, k], uT[:, h, ds(c * CHUNK + k, CHUNK)],
                                       start=(k == 0), stop=(k == TAPS - 1))
                    mm.then_inc(s["gate_conv"], 1)

            def stage2(c, i, b):
                pe.wait_ge(s["scan"], DH * c + DH)
                for j in range(2):
                    ge(pe, s["y"], 2 * (c - 1) + j + 1)
                    for t in (2 * j, 2 * j + 1):
                        for h in range(DH):
                            mm = pe.matmul(Y[j][:, (t % 2) * D:(t % 2 + 1) * D], hT[:, b, h, t * P:(t + 1) * P],
                                           wout[:, h, :], start=(h == 0), stop=(h == DH - 1))
                    mm.then_inc(s["proj"], 1)

            def stage2b(c, i, b):
                ge(pe, s["u2T"], DH * c)
                for mm in transposes(c, lambda t, h: u2[:, t, h * P:(h + 1) * P], s["u2"]):
                    mm.then_inc(s["tr2"], 1)

            def stage3(c, i, b):
                pe.wait_ge(s["u2T"], DH * c + DH)
                ge(pe, s["vt"], TPC * c + 1)
                for q in range(4):
                    if q >= 2:
                        pe.wait_ge(s["res"], 4 * c + q - 1)
                    for h in range(DH):
                        mm = pe.matmul(Q[q % 2][:, :], wqkv[:, h, q * P:(q + 1) * P], u2T[:, h],
                                       start=(h == 0), stop=(h == DH - 1))
                    mm.then_inc(s["qk"], 1)
                for t in range(TPC):
                    if t < 2:
                        pe.wait_ge(s["res"], 4 * c + 3 + t)
                    else:
                        pe.wait_ge(s["vt"], TPC * c + t)
                    for h in range(DH):
                        mm = pe.matmul(Q[t % 2][:, 0:D], u2T[:, h, t * P:(t + 1) * P], wqkv[:, h, 2 * D:3 * D],
                                       start=(h == 0), stop=(h == DH - 1))
                    mm.then_inc(s["v"], 1)

            stages(pe.Fori, stage1, stage2, stage3, stage2b)

        body.close()
        m.clear()


K_PARTS = (0, 0, 0, 1, 1, 2)
Q_PARTS = (0, 1, 2, 0, 1, 0)
ROWS = HD * len(K_PARTS)
SHIFT = 2
VW = 32


def attention_phase(nc, ident, qk_d, v_d, oT_d):
    UNITS = 2 * CHUNKS
    order = list(range(CHUNKS)) + list(range(CHUNKS))[::-1]

    def block_of(n):
        return order[n % UNITS]

    def group_parity(n):
        return n % UNITS // CHUNKS

    steps_before = [4 * sum(block_of(m) + 1 for m in range(n)) for n in range(UNITS + 1)]
    items_before = [16 * sum(block_of(m + 1) + 1 for m in range(n)) for n in range(UNITS + 1)]
    STEP0, UNIT0, ITEM0 = 4, 2, 32

    with ExitStack() as ctx:
        m = Memory(nc, ctx, "a")
        Kt = m.sb("K", [ROWS + SHIFT, 2, GROUP, S], BF16)
        Qt = m.sb("Q", [ROWS + SHIFT, 4, GROUP, CHUNK], BF16)
        Vg = m.sb("Vg", [P, 2, TILES, GROUP * (HD + 1)])
        Vs = m.sb("Vs", [P, 4, GROUP, VW])
        Pt = m.sb("P", [P, 2, GROUP, CHUNK])
        identb = m.sb("identb", [P, P], BF16)
        mask_q = m.sb("mask_q", [P, P], BF16)
        mask_k = m.sb("mask_k", [P, P], BF16)
        ones = m.sb("ones", [P, P], BF16)
        mx = m.sb("mx", [P, 2, CHUNKS, GROUP * TPC])
        top = m.sb("top", [P, GROUP * TPC])
        neg = m.sb("neg", [P, SHIFT, GROUP * TPC], BF16)
        shift = m.sb("shift", [SHIFT * GROUP * TPC, P], BF16)
        osb = m.sb("o", [P, 2, CHUNK])
        ST = m.ps("ST", (P, GROUP, CHUNK))
        O = m.ps("O")
        M = [m.ps(f"M{b}") for b in range(2)]
        turned = m.ps("turned")

        s = {n: m.sem(n) for n in (
            "sp_passed pool_passed ones k_ones k0 k1 v0 v1 q0 q1 q2 q3 setup ident st_a st_b exp_a exp_b pv vs item read top neg negT "
            "shift shift_sent zeroed o o_sent0 o_sent1").split()}
        q_loaded = [s[f"q{b}"] for b in range(4)]
        k_loaded = (s["k0"], s["k1"])
        v_loaded = (s["v0"], s["v1"])
        st_ready = (s["st_a"], s["st_b"])
        exp_done = (s["exp_a"], s["exp_b"])
        o_sent = (s["o_sent0"], s["o_sent1"])
        SETUP = 3
        body = ctx.enter_context(ExitStack())
        block = body.enter_context(nc.Block())

        def first_step(it, n):
            return it * steps_before[UNITS] + (STEP0 + steps_before[n])

        def first_item(it, n):
            return it * items_before[UNITS] + (ITEM0 + items_before[n])

        def unit(it, n):
            return it * UNITS + (UNIT0 + n)

        def walk(eng, it, n, step):
            qi, qm = block_of(n), block_of(n + 1)
            e0, x0 = first_step(it, n), first_item(it, n)

            def four(kk, e, x):
                for j in range(4):
                    step(kk, j, e + j, None if x is None else (x[0], x[1] + 4 * j))
            four(None, e0, (0, x0) if qm else None)
            both = max(0, min(qi, qm - 1))
            if both:
                with eng.Fori(0, both) as kk:
                    four(kk, e0 + 4 + 4 * kk, (kk + 1, x0 + 16 + 16 * kk))
            if qi > both:
                with eng.Fori(both, qi) as kk:
                    four(kk, e0 + 4 + 4 * kk, None)

        def first_col(kk, j):
            return j * P if kk is None else 0

        @block.sync
        def _(sp):
            qk = qk_d.rearrange("s q p n -> s (q p) n")

            def load_k(g, par):
                for b, part in enumerate(K_PARTS):
                    sp.dma_start(Kt[b * HD:(b + 1) * HD, par],
                                 qk[part, ds(D + g * (GROUP * HD), GROUP * HD), :]
                                 .rearrange("(h d) n -> d h n", d=HD)).then_inc(k_loaded[par], 16)
                sp.dma_start(Vg[:, par], v_d[ds(g, 1)].rearrange("o p t h d -> (o p) t (h d)"))\
                  .then_inc(v_loaded[par], 16)

            def load_q(g, n):
                for b, part in enumerate(Q_PARTS):
                    sp.dma_start(Qt[b * HD:(b + 1) * HD, n % 4],
                                 qk[part, ds(g * (GROUP * HD), GROUP * HD),
                                    block_of(n) * CHUNK:(block_of(n) + 1) * CHUNK]
                                 .rearrange("(h d) n -> d h n", d=HD)).then_inc(q_loaded[n % 4], 16)

            load_q(0, 0)
            load_k(0, 0)
            load_q(0, 1)
            load_q(0, 2)
            sp.wait_ge(s["ones"], 1)
            for par in range(2):
                for k in range(SHIFT):
                    sp.dma_start(Kt[ROWS + k:ROWS + k + 1, par].rearrange("o h n -> o (h n)"), ones[:, :])\
                      .then_inc(s["k_ones"], 16)
            with sp.Fori(0, 2) as it:
                for n in range(UNITS):
                    g = it * 2 + n // CHUNKS
                    if n % CHUNKS == 0:
                        pause(sp, s["pv"], first_step(it, n), s["sp_passed"])
                        load_k((g + 1) % GROUPS, 1 - n // CHUNKS)
                    pause(sp, s["pv"], first_step(it, n), s["sp_passed"])
                    n3 = n + 3
                    load_q((it * 2 + n3 // CHUNKS) % GROUPS, n3)
                    pause(sp, s["o"], unit(it, n) + 1, s["sp_passed"])
                    for h in range(GROUP):
                        sp.dma_start(oT_d[:, ds(g * GROUP + h, 1), block_of(n) * CHUNK:(block_of(n) + 1) * CHUNK]
                                     .rearrange("d o n -> (d o) n"),
                                     osb[h * VW:h * VW + HD + 1, n % 2]).then_inc(o_sent[n % 2], 16)
            for b in range(2):
                sp.wait_ge(o_sent[b], 64 * UNITS + 16)
            for b in range(4):
                sp.wait_ge(q_loaded[b], 96 * (2 * UNITS // 4 + (b < 3)))
            for b in range(2):
                sp.wait_ge(k_loaded[b], 96 * (GROUPS // 2 + (b == 0)))
                sp.wait_ge(v_loaded[b], 16 * (GROUPS // 2 + (b == 0)))

        @block.gpsimd
        def _(pool):
            pool.memset(identb[:, :], 0.0).then_inc(s["ident"], 1)
            pool.memset(mask_q[:, :], 0.0).then_inc(s["ident"], 1)
            pool.memset(mask_k[:, :], 0.0).then_inc(s["ident"], 1)
            pool.memset(Vs[:, :, :, :], 0.0).then_inc(s["ident"], 1)
            pool.wait_ge(s["ident"], 4)
            pool.affine_select(out=identb[:, :], in_=identb[:, :], compare_op=ALU.not_equal, fill=1.0, base=0,
                               pattern=[[-1, P]], channel_multiplier=1).then_inc(s["setup"], 1)
            pool.affine_select(out=mask_q[:, :], in_=mask_q[:, :], compare_op=ALU.is_ge, fill=MASKED, base=0,
                               pattern=[[-1, P]], channel_multiplier=1).then_inc(s["setup"], 1)
            pool.affine_select(out=mask_k[:, :], in_=mask_k[:, :], compare_op=ALU.is_ge, fill=MASKED, base=0,
                               pattern=[[1, P]], channel_multiplier=-1).then_inc(s["setup"], 1)
            pool.sem_inc(s["zeroed"], UNIT0)
            pool.sem_inc(s["vs"], STEP0)
            with pool.Fori(0, 2) as it:
                for n in range(UNITS):
                    if n % CHUNKS == 0:
                        pause(pool, v_loaded[n // CHUNKS], 16 * it + 16, s["pool_passed"])

                    def step(kk, j, e, beside):
                        pause(pool, s["pv"], e - 3, s["pool_passed"])
                        at = block_of(n) * 4 + j if kk is None else 4 * kk + j
                        pool.tensor_copy(Vs[:, j, :, 0:HD + 1],
                                         Vg[:, group_parity(n), ds(at, 1), :]
                                         .rearrange("p o (h d) -> p (o h) d", h=GROUP)).then_inc(s["vs"], 1)
                        if kk is None and j == 3:
                            pause(pool, s["pv"], e - 1, s["pool_passed"])
                            pool.memset(Pt[:, 1, :, 0:3 * P], 0.0).then_inc(s["zeroed"], 1)
                    walk(pool, it, n, step)

        @block.scalar
        def _(act):
            for e in exp_done:
                act.sem_inc(e, STEP0)
            act.sem_inc(s["o"], UNIT0)
            act.sem_inc(s["shift"], UNIT0)

            def send_shift(u, n):
                act.wait_ge(s["negT"], u + 1)
                act.wait_ge(s["shift_sent"], 16 * SHIFT * u)
                act.copy(shift[:, :], turned[0:SHIFT * GROUP * TPC, 0:P // 2].bitcast(BF16)).then_inc(s["shift"], 1)
                act.wait_ge(s["shift"], u + 1)
                for k in range(SHIFT):
                    act.dma_start(Qt[ROWS + k:ROWS + k + 1, n % 4].rearrange("o h q -> o (h q)"),
                                  shift[k * 16:(k + 1) * 16, :]).then_inc(s["shift_sent"], 16)

            act.sem_inc(s["shift_sent"], 16 * SHIFT * UNIT0)
            send_shift(UNIT0, 0)
            with act.Fori(0, 2) as it:
                for n in range(UNITS):
                    def step(kk, j, e, beside):
                        c0 = first_col(kk, j)
                        act.wait_ge(s["pv"], e - 1)
                        for half in range(2):
                            hs = slice(2 * half, 2 * half + 2)
                            act.wait_ge(st_ready[half], e + 1)
                            act.activation(Pt[:, j % 2, hs, c0:], ST[:, hs, c0:], ACT.Exp, scale=HD ** -0.5)\
                               .then_inc(exp_done[half], 1)
                    walk(act, it, n, step)
                    send_shift(unit(it, n) + 1, n + 1)
                    act.wait_ge(s["pv"], first_step(it, n + 1))
                    act.wait_ge(o_sent[n % 2], it * (64 * CHUNKS) + 64 * (n // 2) + 16)
                    act.copy(osb[:, n % 2], O[:, :]).then_inc(s["o"], 1)
            act.wait_ge(s["shift_sent"], 16 * SHIFT * (UNIT0 + 1 + 2 * UNITS))

        @block.vector
        def _(dve):
            dve.memset(ones[:, :], 1.0).then_inc(s["ones"], 1)

            def read(n, slot, t, h, x, cols):
                dve.wait_ge(s["item"], x + 1)
                dve.tensor_reduce(mx[:, n % 2, ds(slot, 1), h * TPC + t:h * TPC + t + 1]
                                  .rearrange("p a b -> p (a b)"), M[(4 * t + h) % 2][:, 0:cols], AX.X, ALU.max)\
                   .then_inc(s["read"], 1)

            def diagonal(n, x0):
                for t in range(TPC):
                    for h in range(GROUP):
                        read(n, 0, t, h, x0 + (4 * t + h), (t + 1) * P)

            def finish(n, u, x):
                dve.wait_ge(s["read"], x)
                dve.tensor_reduce(top[:, :], mx[:, n % 2, 0:block_of(n) + 1].rearrange("p k i -> p i k"),
                                  AX.X, ALU.max).then_inc(s["top"], 1)
                dve.wait_ge(s["top"], u - UNIT0 + 1)
                if not (isinstance(u, int)):
                    dve.wait_ge(s["negT"], u)
                dve.tensor_scalar(neg[:, 0], top[:, :], -1.0, None, ALU.mult).then_inc(s["neg"], 1)
                dve.wait_ge(s["neg"], 2 * (u - UNIT0) + 1)
                dve.scalar_tensor_tensor(neg[:, 1], top[:, :], -1.0, neg[:, 0], ALU.mult, ALU.subtract)\
                   .then_inc(s["neg"], 1)

            diagonal(0, 0)
            finish(0, UNIT0, 16)
            diagonal(1, 16)
            with dve.Fori(0, 2) as it:
                for n in range(UNITS):
                    def step(kk, j, e, beside):
                        for h in range(GROUP if beside else 0):
                            read(n + 1, beside[0] + 1, j, h, beside[1] + h, CHUNK)
                    walk(dve, it, n, step)
                    x = first_item(it, n) + 16 * block_of(n + 1)
                    finish(n + 1, unit(it, n) + 1, x)
                    diagonal(n + 2, x)

        @block.tensor
        def _(pe):
            for e in (*st_ready, s["pv"]):
                pe.sem_inc(e, STEP0)
            pe.sem_inc(s["negT"], UNIT0)
            pe.sem_inc(o_sent[0], 16)
            pe.sem_inc(o_sent[1], 16)

            def scores(n, kk, j, e, half):
                c0 = first_col(kk, j)
                par = group_parity(n)
                at = block_of(n) * CHUNK + j * P if kk is None else kk * CHUNK + j * P
                pe.wait_ge(exp_done[half], e)
                for h in (2 * half, 2 * half + 1):
                    mm = pe.matmul(ST[:, h, c0:], Kt[:, par, h, ds(at, P)], Qt[:, n % 4, h, c0:],
                                   start=True, stop=kk is not None)
                    if kk is None:
                        mm = pe.matmul(ST[:, h, c0:c0 + P], identb[:, :], mask_k[:, :], start=False, stop=True)
                mm.then_inc(st_ready[half], 1)

            def values(n, diag, j, e, between=None):
                pe.wait_ge(exp_done[0], e + 1)
                pe.wait_ge(exp_done[1], e + 1)
                pe.wait_ge(s["vs"], e + 1)
                first = diag and j == 0
                c0 = j * P if diag else 0
                cut = c0 if first else max(c0, CHUNK // 2)
                for cols in (slice(c0, cut), slice(cut, CHUNK)):
                    if cols.start == cols.stop:
                        continue
                    for h in range(GROUP):
                        mm = pe.matmul(O[h * VW:(h + 1) * VW, cols], Vs[:, j, h], Pt[:, j % 2, h, cols],
                                       start=first, stop=True, skip_group_check=True)
                    if between and cols.stop < CHUNK:
                        between()
                        between = None
                mm.then_inc(s["pv"], 1)
                if between:
                    between()

            def ready(x):
                ge(pe, s["read"], x - 1)

            def full_item(n, kk, t, h, x):
                ready(x)
                pe.matmul(M[(4 * t + h) % 2][:, :], Qt[0:ROWS, n % 4, h, t * P:(t + 1) * P],
                          Kt[0:ROWS, group_parity(n), h, ds(kk * CHUNK, CHUNK)], start=True, stop=True)\
                  .then_inc(s["item"], 1)

            def diagonal(n, x0, ts=range(TPC)):
                for t in ts:
                    for h in range(GROUP):
                        ready(x0 + (4 * t + h))
                        b = M[(4 * t + h) % 2]
                        at = block_of(n) * CHUNK
                        pe.matmul(b[:, 0:(t + 1) * P], Qt[0:ROWS, n % 4, h, t * P:(t + 1) * P],
                                  Kt[0:ROWS, group_parity(n), h, at:at + (t + 1) * P], start=True, stop=False)
                        pe.matmul(b[:, t * P:(t + 1) * P], identb[:, :], mask_q[:, :], start=False, stop=True)\
                          .then_inc(s["item"], 1)

            def turn(u):
                pe.wait_ge(s["neg"], 2 * (u - UNIT0) + 2)
                if not isinstance(u, int):
                    pe.wait_ge(s["shift"], u)
                pe.transpose(turned[0:SHIFT * GROUP * TPC, 0:P // 2].bitcast(BF16),
                             neg[:, :, :].rearrange("p k i -> p (k i)"), identb[:, :]).then_inc(s["negT"], 1)

            pe.wait_ge(s["setup"], SETUP)
            pe.wait_ge(q_loaded[0], 96)
            pe.wait_ge(k_loaded[0], 96)
            diagonal(0, 0)
            turn(UNIT0)
            pe.wait_ge(q_loaded[1], 96)
            diagonal(1, 16)
            pe.wait_ge(s["k_ones"], 64 * SHIFT // 2)
            with pe.Fori(0, 2) as it:
                for n in range(UNITS):
                    u = unit(it, n)
                    pe.wait_ge(s["shift_sent"], 16 * SHIFT * (u + 1))

                    def step(kk, j, e, beside):
                        def item(h):
                            if beside:
                                full_item(n + 1, beside[0], j, h, beside[1] + h)
                        scores(n, kk, j, e, 0)
                        item(0)
                        scores(n, kk, j, e, 1)
                        item(1)
                        if kk is None and j == 1:
                            pe.wait_ge(s["o"], u)
                        if kk is not None and j == 0:
                            pe.wait_ge(s["zeroed"], u + 1)
                        if kk is not None or j:
                            values(n, kk is None, (j - 1) % 4, e - 1, between=lambda: item(2))
                        else:
                            item(2)
                        item(3)
                    walk(pe, it, n, step)
                    x = first_item(it, n) + 16 * block_of(n + 1)
                    pe.wait_ge(q_loaded[(n + 2) % 4], it * (96 * UNITS // 4) + 96 * ((n + 2) // 4 + 1))
                    if (n + 2) % CHUNKS == 0:
                        pe.wait_ge(k_loaded[group_parity(n + 2)], it * 96 + 96 * ((n + 2) // UNITS + 1))
                    diagonal(n + 2, x, range(2))
                    turn(u + 1)
                    pe.wait_ge(s["zeroed"], u + 1)
                    values(n, block_of(n) == 0, 3, first_step(it, n + 1) - 1)
                    diagonal(n + 2, x, range(2, TPC))

        body.close()
        m.clear()


PLACES = 2 * P
RPT = PLACES // P
TILE_SLOTS = 2 * S // PLACES + EXPERTS


def route_phase(nc, ident, oT_d, rz_d, u2_d, w_o, g1, b1, wg, h_d, places_d, place, weight, expert_of):
    COUNTED, ROUTED = 19, 37
    with ExitStack() as ctx:
        m = Memory(nc, ctx, "r")
        zs = m.sb("zs", [P, CHUNK])
        rz = m.sb("rz", [P, S])
        oT = m.sb("oT", [P, 2, DH, CHUNK])
        oN = m.sb("oN", [P, 2, DH, CHUNK])
        u2 = m.sb("u2", [P, 2, TPC, D])
        wo = m.sb("wo", [P, DH, D])
        wgs = m.sb("wg", [P, DH, EXPERTS])
        rows = m.sb("rows", [P, 2, D])
        a = m.sb("a", [P, TPC, D])
        hn = m.sb("hn", [P, TPC, D])
        hg = m.sb("hg", [P, TPC, D])
        hs = m.sb("h", [P, 2, TPC, D])
        H = m.sb("H", [P, TILES, D])
        hT = m.sb("hT", [P, DH, CHUNK])
        st = m.sb("st", [P, TPC, 6])
        mv = m.sb("mv", [P, TPC, 2])
        sm = m.sb("sm", [P, 3, TPC])
        L = m.sb("L", [P, TILES, EXPERTS])
        w = {n: m.sb(n, [P, TILES, EXPERTS]) for n in "e iota eq one1 one2 both pre t0 t1".split()}
        v = {n: m.sb(n, [P, TILES]) for n in "top1 top2 sum i1 i2 p1 p2".split()}
        zero = m.sb("zero", [P, D])
        tri = m.sb("tri", [P, P])
        one = m.sb("one", [P, P])
        cnt = m.sb("cnt", [P, EXPERTS])
        tot = m.sb("tot", [P, 6, EXPERTS])
        grid = m.sb("grid", [P, EXPERTS, TILES])
        gridc = m.sb("gridc", [P, EXPERTS, TILES])
        tl = m.sb("tl", [P, TILE_SLOTS, EXPERTS])
        tlc = m.sb("tlc", [P, TILE_SLOTS, EXPERTS])
        ef = m.sb("ef", [P, TILE_SLOTS])
        Y = [m.ps(f"Y{j}") for j in range(2)]
        T = [m.ps(f"T{h}") for h in range(DH)]
        G = m.ps("G")

        s = {n: m.sem(n) for n in (
            "passed z_in rz_done rz_out rz_in in0 in1 consts oN proj a st mv a1 sd a2 hn hg h h_out0 h_out1 tr hT gate L setup "
            "rt exp pre pre_mm zero zeroed sent").split()}
        loaded = (s["in0"], s["in1"])
        h_out = (s["h_out0"], s["h_out1"])
        consts = [(wo[:, :, :], None), (wgs[:, :, :], wg.rearrange("(h p) e -> p h e", p=P)),
                  (rows[:, 0], g1.partition_broadcast(P)), (rows[:, 1], b1.partition_broadcast(P))]
        CONSTS = 16 * (len(consts))
        body = ctx.enter_context(ExitStack())
        block = body.enter_context(nc.Block())

        def chunks(fori, first, second):
            def pair(i):
                for b in range(2):
                    first(2 * i + (1 + b), 1 - b)
                    second(2 * i + b, b)
            first(0, 0)
            pair(0)
            with fori(1, CHUNKS // 2 - 1) as i:
                pair(i)
            first(CHUNKS - 1, 1)
            second(CHUNKS - 2, 0)
            second(CHUNKS - 1, 1)

        def nothing(c, b):
            pass

        @block.sync
        def _(sp):
            sp.dma_start(zs[:, :], oT_d[HD].rearrange("h (c n) -> (h c) n", n=CHUNK)).then_inc(s["z_in"], 16)
            sp.dma_start(wo[:, :, :], w_o.rearrange("(h p) e -> p h e", p=P)).then_inc(s["consts"], 16)
            for dst, src in consts[1:]:
                sp.dma_start(dst, src).then_inc(s["consts"], 16)
            sp.wait_ge(s["rz_done"], 1)
            sp.dma_start(rz_d.rearrange("h (c n) -> (h c) n", n=CHUNK), zs[:, :]).then_inc(s["rz_out"], 16)
            sp.wait_ge(s["rz_out"], 16)
            sp.dma_start(rz[:, :], rz_d.partition_broadcast(P // HEADS)).then_inc(s["rz_in"], 16)

            def load(c, b):
                ge(sp, s["a"], 2 * (c - 1))
                ge(sp, s["oN"], c - 1)
                for h in range(DH):
                    sp.dma_start(oT[:, b, h],
                                 oT_d[h * (HD // DH):(h + 1) * (HD // DH), :, ds(c * CHUNK, CHUNK)]
                                 .rearrange("d h n -> (d h) n")).then_inc(loaded[b], 16)
                sp.dma_start(u2[:, b], u2_d.rearrange("(t p) d -> p t d", p=P)[:, ds(c * TPC, TPC), :])\
                  .then_inc(loaded[b], 16)

            def store(c, b):
                sp.wait_ge(s["h"], c + 1)
                sp.dma_start(h_d.rearrange("(t p) d -> p t d", p=P)[:, ds(c * TPC, TPC), :], hs[:, b])\
                  .then_inc(h_out[b], 16)
            load(0, 0)
            load(1, 1)
            store(0, 0)
            load(2, 0)
            store(1, 1)
            with sp.Fori(1, CHUNKS // 2 - 1) as i:
                for b in range(2):
                    load(2 * i + (1 + b), 1 - b)
                    store(2 * i + b, b)
            load(CHUNKS - 1, 1)
            store(CHUNKS - 2, 0)
            store(CHUNKS - 1, 1)
            for b in range(2):
                sp.wait_ge(h_out[b], 16 * CHUNKS // 2)

        @block.gpsimd
        def _(pool):
            pool.memset(zero[:, :], 0.0).then_inc(s["zero"], 1)
            pool.memset(tri[:, :], 1.0).then_inc(s["zero"], 1)
            pool.memset(one[:, :], 1.0).then_inc(s["setup"], 1)
            pool.wait_ge(s["zero"], 2)
            for k in range(RPT * TILE_SLOTS // 8):
                pool.dma_start(places_d.rearrange("(t p) d -> p t d", p=P)[:, 8 * k:8 * k + 8, :],
                               zero[:, :].unsqueeze(1).broadcast_to([P, 8, D])).then_inc(s["zeroed"], 16)
            pool.affine_select(out=tri[:, :], in_=tri[:, :], compare_op=ALU.is_gt, fill=0.0, base=0,
                               pattern=[[1, P]], channel_multiplier=-1).then_inc(s["setup"], 1)
            for k, (t, pattern) in enumerate(((w["iota"], [[0, TILES], [1, EXPERTS]]),
                                              (grid, [[0, EXPERTS], [PLACES, TILES]]),
                                              (tl, [[1, TILE_SLOTS], [0, EXPERTS]]))):
                pool.iota(t[:, :, :], pattern=pattern, base=0, channel_multiplier=0,
                          allow_small_or_imprecise_dtypes=True).then_inc(s["setup"], 1)

            def norm(c, b):
                ge(pool, h_out[b], 8 * (c - b))
                pool.wait_ge(s["hn"], TPC * c + TPC)
                ge(pool, s["h"], c)
                pool.tensor_tensor(hg[:, :, :], hn[:, :, :], rows[:, 0].unsqueeze(1).broadcast_to([P, TPC, D]),
                                   ALU.mult).then_inc(s["hg"], 1)
                pool.wait_ge(s["hg"], c + 1)
                ge(pool, s["tr"], DH * (c - 1))
                ge(pool, s["L"], 2 * (c - 1))
                pool.tensor_tensor(hs[:, b], hg[:, :, :], rows[:, 1].unsqueeze(1).broadcast_to([P, TPC, D]),
                                   ALU.add).then_inc(s["h"], 1)
            pool.wait_ge(s["consts"], CONSTS)
            chunks(pool.Fori, norm, nothing)
            pool.wait_ge(s["zeroed"], 16 * (RPT * TILE_SLOTS // 8))
            pool.wait_ge(s["rt"], ROUTED)
            pool.wait_ge(s["L"], 2 * CHUNKS)
            for t in range(TILES):
                for k in range(2):
                    pool.indirect_dma_start(places_d, bass.IndirectOffsetOnAxis(place[:, k, t:t + 1], 0), H[:, t],
                                            None).then_inc(s["sent"], 16)
            pool.wait_ge(s["sent"], 16 * 2 * TILES)

        @block.scalar
        def _(act):
            def first(c, b):
                act.wait_ge(s["a1"], c + 1)
                act.activation(sm[:, 1], sm[:, 0], ACT.Sqrt).then_inc(s["sd"], 1)

            def second(c, b):
                for h in range(DH):
                    act.wait_ge(s["tr"], DH * c + (h + 1))
                    ge(act, s["gate"], TPC * c)
                    act.copy(hT[:, h], T[h][:, :]).then_inc(s["hT"], 1)
                act.wait_ge(s["h"], c + 1)
                act.copy(H[:, ds(c * TPC, TPC), :], hs[:, b]).then_inc(s["L"], 1)
                act.wait_ge(s["gate"], TPC * c + TPC)
                act.copy(L[:, ds(c * TPC, TPC), :],
                         G[:, 0:TPC * EXPERTS].rearrange("p (t e) -> p t e", e=EXPERTS)).then_inc(s["L"], 1)
            chunks(act.Fori, first, second)
            act.wait_ge(s["rt"], 2)
            act.activation(w["e"][:, :, :], w["e"][:, :, :], ACT.Exp).then_inc(s["exp"], 1)

        @block.vector
        def _(dve):
            dve.wait_ge(s["z_in"], 16)
            dve.reciprocal(zs[:, :], zs[:, :]).then_inc(s["rz_done"], 1)
            dve.wait_ge(s["rz_in"], 16)

            def first(c, b):
                dve.wait_ge(loaded[b], 24 * (c - b) + 48)
                ge(dve, s["proj"], 2 * (c - 1))
                dve.tensor_tensor(oN[:, b], oT[:, b],
                                  rz[:, ds(c * CHUNK, CHUNK)].unsqueeze(1).broadcast_to([P, DH, CHUNK]), ALU.mult)\
                   .then_inc(s["oN"], 1)
                ge(dve, s["hn"], TPC * c)
                for j in range(2):
                    dve.wait_ge(s["proj"], 2 * c + (j + 1))
                    dve.tensor_tensor(a[:, 2 * j:2 * j + 2].rearrange("p t d -> p (t d)"), Y[j][:, :],
                                      u2[:, b, 2 * j:2 * j + 2].rearrange("p t d -> p (t d)"), ALU.add)\
                       .then_inc(s["a"], 1)
                for t in range(TPC):
                    if t % 2 == 0:
                        dve.wait_ge(s["a"], 2 * c + (t // 2 + 1))
                    dve.bn_stats(st[:, t], a[:, t]).then_inc(s["st"], 1)
                pause(dve, s["st"], TPC * c + TPC, s["passed"])
                for t in range(TPC):
                    dve.bn_aggr(mv[:, t], st[:, t]).then_inc(s["mv"], 1)
                dve.wait_ge(s["mv"], TPC * c + TPC)
                dve.tensor_scalar(sm[:, 0], mv[:, :, 1], LN_EPS, None, ALU.add).then_inc(s["a1"], 1)
                dve.wait_ge(s["sd"], c + 1)
                dve.reciprocal(sm[:, 2], sm[:, 1]).then_inc(s["a2"], 1)
                dve.wait_ge(s["a2"], c + 1)
                ge(dve, s["hg"], c)
                for t in range(TPC):
                    dve.tensor_scalar(hn[:, t], a[:, t], mv[:, t, 0:1], sm[:, 2, t:t + 1], ALU.subtract, ALU.mult)\
                       .then_inc(s["hn"], 1)
            chunks(dve.Fori, first, nothing)

            n = [0]

            def did(ins):
                ins.then_inc(s["rt"], 1)
                n[0] += 1
                dve.wait_ge(s["rt"], n[0])

            def spread(x):
                return x.unsqueeze(2).broadcast_to([P, TILES, EXPERTS])
            dve.wait_ge(s["L"], 2 * CHUNKS)
            did(dve.tensor_reduce(v["top1"][:, :], L[:, :, :], AX.X, ALU.max))
            did(dve.tensor_tensor(w["e"][:, :, :], L[:, :, :], spread(v["top1"][:, :]), ALU.subtract))
            dve.wait_ge(s["exp"], 1)
            dve.wait_ge(s["setup"], 5)
            for k in (1, 2):
                top, i, one_hot = v[f"top{k}"], v[f"i{k}"], w[f"one{k}"]
                did(dve.tensor_reduce(top[:, :], w["e"][:, :, :], AX.X, ALU.max))
                did(dve.tensor_tensor(w["eq"][:, :, :], w["e"][:, :, :], spread(top[:, :]), ALU.is_lt))
                did(dve.scalar_tensor_tensor(w["eq"][:, :, :], w["eq"][:, :, :], float(EXPERTS),
                                             w["iota"][:, :, :], ALU.mult, ALU.add))
                did(dve.tensor_reduce(i[:, :], w["eq"][:, :, :], AX.X, ALU.min))
                did(dve.tensor_tensor(one_hot[:, :, :], w["iota"][:, :, :], spread(i[:, :]), ALU.is_equal))
                if k == 1:
                    did(dve.scalar_tensor_tensor(w["e"][:, :, :], one_hot[:, :, :], -2.0, w["e"][:, :, :],
                                                 ALU.mult, ALU.add))
            did(dve.tensor_tensor(v["sum"][:, :], v["top1"][:, :], v["top2"][:, :], ALU.add))
            did(dve.reciprocal(v["sum"][:, :], v["sum"][:, :]))
            did(dve.tensor_tensor(weight[:, 0], v["top1"][:, :], v["sum"][:, :], ALU.mult))
            did(dve.tensor_tensor(weight[:, 1], v["top2"][:, :], v["sum"][:, :], ALU.mult))
            did(dve.tensor_tensor(w["both"][:, :, :], w["one1"][:, :, :], w["one2"][:, :, :], ALU.add))
            for e in range(EXPERTS):
                scan = dve.tensor_tensor_scan(out=w["pre"][:, :, e], data0=one[:, 0:TILES],
                                              data1=w["both"][:, :, e], initial=0.0, op0=ALU.mult, op1=ALU.add)
                scan.then_inc(s["pre"], 1)
            dve.wait_ge(s["pre"], EXPERTS)
            did(dve.tensor_copy(cnt[:, :], w["pre"][:, TILES - 1, :]))
            dve.wait_ge(s["pre_mm"], 1)
            did(dve.tensor_copy(tot[:, 0], G[:, 0:EXPERTS]))
            did(dve.tensor_copy(tot[:, 1], G[:, EXPERTS:2 * EXPERTS]))
            did(dve.tensor_tensor(gridc[:, :, :], grid[:, :, :],
                                  tot[:, 1].unsqueeze(2).broadcast_to([P, EXPERTS, TILES]), ALU.is_lt))
            did(dve.tensor_reduce(tot[:, 2], gridc[:, :, :], AX.X, ALU.add))
            did(dve.tensor_tensor_scan(out=tot[:, 3], data0=one[:, 0:EXPERTS], data1=tot[:, 2], initial=0.0,
                                       op0=ALU.mult, op1=ALU.add))
            did(dve.tensor_tensor(tot[:, 4], tot[:, 3], tot[:, 2], ALU.subtract))
            did(dve.scalar_tensor_tensor(tot[:, 5], tot[:, 4], float(PLACES), tot[:, 0], ALU.mult, ALU.add))
            did(dve.tensor_tensor(w["t0"][:, :, :], w["pre"][:, :, :], w["both"][:, :, :], ALU.subtract))
            did(dve.tensor_tensor(w["t1"][:, :, :], w["t0"][:, :, :],
                                  tot[:, 5].unsqueeze(1).broadcast_to([P, TILES, EXPERTS]), ALU.add))
            for k in (1, 2):
                did(dve.tensor_tensor(w["t0"][:, :, :], w["t1"][:, :, :], w[f"one{k}"][:, :, :], ALU.mult))
                did(dve.tensor_reduce(v[f"p{k}"][:, :], w["t0"][:, :, :], AX.X, ALU.add))
                did(dve.tensor_copy(place[:, k - 1], v[f"p{k}"][:, :]))
            did(dve.tensor_tensor(tlc[:, :, :], tl[:, :, :],
                                  tot[:, 3].unsqueeze(1).broadcast_to([P, TILE_SLOTS, EXPERTS]), ALU.is_ge))
            did(dve.tensor_reduce(ef[:, :], tlc[:, :, :], AX.X, ALU.add))
            did(dve.tensor_scalar(expert_of[:, :], ef[:, :], float(EXPERTS - 1), None, ALU.min))
            assert n[0] == ROUTED, n

        @block.tensor
        def _(pe):
            pe.wait_ge(s["consts"], CONSTS)

            def first(c, b):
                pe.wait_ge(s["oN"], c + 1)
                for j in range(2):
                    ge(pe, s["a"], 2 * (c - 1) + (j + 1))
                    for t in (2 * j, 2 * j + 1):
                        for h in range(DH):
                            mm = pe.matmul(Y[j][:, (t % 2) * D:(t % 2 + 1) * D], oN[:, b, h, t * P:(t + 1) * P],
                                           wo[:, h, :], start=(h == 0), stop=(h == DH - 1))
                    mm.then_inc(s["proj"], 1)

            def second(c, b):
                pe.wait_ge(s["h"], c + 1)
                ge(pe, s["hT"], DH * c)
                for h in range(DH):
                    for t in range(TPC):
                        mm = pe.transpose(T[h][:, t * P:(t + 1) * P], hs[:, b, t, h * P:(h + 1) * P], ident[:, :])
                    mm.then_inc(s["tr"], 1)
                pe.wait_ge(s["hT"], DH * c + DH)
                ge(pe, s["L"], 2 * c)
                for t in range(TPC):
                    for h in range(DH):
                        mm = pe.matmul(G[:, t * EXPERTS:(t + 1) * EXPERTS], hT[:, h, t * P:(t + 1) * P], wgs[:, h, :],
                                       start=(h == 0), stop=(h == DH - 1))
                    mm.then_inc(s["gate"], 1)
            chunks(pe.Fori, first, second)
            pe.wait_ge(s["setup"], 5)
            pe.wait_ge(s["rt"], COUNTED)
            pe.matmul(G[:, 0:EXPERTS], tri[:, :], cnt[:, :], start=True, stop=True)
            pe.matmul(G[:, EXPERTS:2 * EXPERTS], one[:, :], cnt[:, :], start=True, stop=True).then_inc(s["pre_mm"], 1)

        body.close()
        m.clear()


W_SCALE = 64.0


def expert_phase(nc, ident, places_d, w1, bb1, w2, bb2, expert_of, ys_d):
    AHEAD = 4
    BANKS = 4
    FPB = FB // BANKS
    HALF = FB // 2
    with ExitStack() as ctx:
        m = Memory(nc, ctx, "e")
        stage = m.sb("stage", [P, 2, 2, DH * F])
        W1 = m.sb("W1", [P, 2, EXPERTS * DH, F], F16)
        W2 = m.sb("W2", [P, 2, EXPERTS * FB, D], F16)
        bias1 = m.sb("bias1", [P, EXPERTS * FB])
        bias2 = m.sb("bias2", [P, EXPERTS, D])
        x = m.sb("x", [P, 2, RPT, D])
        xT = m.sb("xT", [P, 2, 2, DH, PLACES], F16)
        g = m.sb("g", [P, FB, PLACES])
        gT = m.sb("gT", [P, 2, 2, FB, PLACES], F16)
        y = m.sb("y", [P, 2, RPT, D])
        T = [m.ps(f"T{b}", (P, DH, PLACES)) for b in range(2)]
        Hb = [m.ps(f"H{k}", (P, FPB, PLACES)) for k in range(BANKS)]
        Y = [m.ps(f"Y{b}", (P, RPT, D)) for b in range(2)]

        s = {n: m.sem(n) for n in (
            "consts w00 w01 w10 w11 v00 v01 v10 v11 sc1 sc2 hi1 hi2 lo1 lo2 x0 x1 tr xh xl up gelu gh gl down y y_out0 y_out1").split()}
        wload = ((s["w00"], s["w01"]), (s["w10"], s["w11"]))
        later = ((s["v00"], s["v01"]), (s["v10"], s["v11"]))
        x_in = (s["x0"], s["x1"])
        y_out = (s["y_out0"], s["y_out1"])
        scaled, hi, lo = ((s[f"{n}1"], s[f"{n}2"]) for n in ("sc", "hi", "lo"))
        body = ctx.enter_context(ExitStack())
        block = body.enter_context(nc.Block())

        def tiles(fori, *stages):
            def step(t, b):
                for work, lag in stages:
                    if not isinstance(t, int):
                        work(t + lag, (b + lag) % 2)
                    elif 0 <= t + lag < TILE_SLOTS:
                        work(t + lag, (b + lag) % 2)
            for t in range(-AHEAD, 2):
                step(t, t % 2)
            with fori(1, (TILE_SLOTS - AHEAD) // 2) as i:
                for b in range(2):
                    step(2 * i + b, b)
            for t in range(TILE_SLOTS - AHEAD, TILE_SLOTS + 1):
                step(t, t % 2)

        def expert(eng, t):
            return eng.value_load(expert_of[0:1, ds(t, 1)], min_val=0, max_val=EXPERTS - 1)

        def weights(e, k):
            W, n = ((W1, DH), (W2, FB))[k]
            return (stage[:, e % 2, k].rearrange("p (a b) -> p a b", a=n),
                    W[:, 0, e * n:(e + 1) * n, :], W[:, 1, e * n:(e + 1) * n, :])

        def load_weights(eng, e, k):
            src = (w1[e].rearrange("(h p) f -> p h f", p=P), w2[e].rearrange("(k p) d -> p k d", p=P))[k]
            eng.dma_start(weights(e, k)[0], src).then_inc((wload if e < 2 else later)[e % 2][k], 16)

        @block.sync
        def _(sp):
            def load(t, b):
                ge(sp, s["tr"], t - 1)
                sp.dma_start(x[:, b], places_d[ds(t * PLACES, PLACES), :].rearrange("(q p) d -> p q d", p=P))\
                  .then_inc(x_in[b], 16)
                if isinstance(t, int) and t < 2:
                    for k in range(2):
                        load_weights(sp, t, k)
                if isinstance(t, int) and t == 1:
                    sp.dma_start(bias1[:, :], bb1).then_inc(s["consts"], 16)
                    sp.dma_start(bias2[:, :, :], bb2.partition_broadcast(P)).then_inc(s["consts"], 16)

            def store(t, b):
                sp.wait_ge(s["y"], t + 1)
                sp.dma_start(ys_d[ds(t * PLACES, PLACES), :].rearrange("(q p) d -> p q d", p=P), y[:, b])\
                  .then_inc(y_out[b], 16)
            tiles(sp.Fori, (load, AHEAD), (store, -1))
            for b in range(2):
                sp.wait_ge(y_out[b], 8 * TILE_SLOTS)

        def split_on_pool(pool, e, k):
            whole, high, low = weights(e, k)
            pool.wait_ge(later[e % 2][k], 16 * (e // 2))
            pool.tensor_scalar(whole, whole, W_SCALE, None, ALU.mult).then_inc(scaled[k], 1)
            pool.wait_ge(scaled[k], e - 1)
            pool.tensor_copy(high, whole).then_inc(hi[k], 1)
            pool.wait_ge(hi[k], e + 1)
            pool.wait_ge(lo[k], e)
            pool.tensor_tensor(low, whole, high, ALU.subtract).then_inc(lo[k], 1)

        @block.gpsimd
        def _(pool):
            for e in range(2, EXPERTS):
                for k in range(2):
                    pool.wait_ge(lo[k], e - 1)
                    load_weights(pool, e, k)
                if e == 2:
                    continue
                for k in range(2):
                    split_on_pool(pool, e - 1, k)
            for k in range(2):
                split_on_pool(pool, EXPERTS - 1, k)

        @block.scalar
        def _(act):
            for e in range(2):
                for k in range(2):
                    whole, high, low = weights(e, k)
                    act.wait_ge(wload[e][k], 16)
                    act.activation(high, whole, ACT.Copy, scale=W_SCALE).then_inc(hi[k], 1)
            act.wait_ge(s["consts"], 32)

            def split(t, b):
                act.wait_ge(s["tr"], t + 1)
                ge(act, s["up"], BANKS * (t - 1))
                act.copy(xT[:, b, 0], T[b][:, :, :]).then_inc(s["xh"], 1)

            def gelu(t, b):
                e = expert(act, t)
                for f in range(FB):
                    if f % FPB == 0:
                        act.wait_ge(s["up"], BANKS * t + (f // FPB + 1))
                    if f % HALF == 0:
                        ge(act, s["gl"], 2 * (t - 1) + (f // HALF + 1))
                    act.activation(g[:, f], Hb[f // FPB][:, f % FPB], ACT.Gelu_apprx_tanh,
                                   bias=bias1[:, ds(e * FB + f, 1)], scale=1 / W_SCALE).then_inc(s["gelu"], 1)
            tiles(act.Fori, (gelu, 0), (split, 2))

        @block.vector
        def _(dve):
            for e in range(2):
                for k in range(2):
                    whole, high, low = weights(e, k)
                    dve.wait_ge(hi[k], e + 1)
                    dve.scalar_tensor_tensor(low, whole, W_SCALE, high, ALU.mult, ALU.subtract).then_inc(lo[k], 1)
            dve.wait_ge(s["consts"], 32)

            def split(t, b):
                dve.wait_ge(s["xh"], t + 1)
                dve.tensor_tensor(xT[:, b, 1], T[b][:, :, :], xT[:, b, 0], ALU.subtract).then_inc(s["xl"], 1)

            def split_gelu(t, b):
                ge(dve, s["down"], t - 1)
                for j in range(2):
                    part = slice(j * HALF, (j + 1) * HALF)
                    dve.wait_ge(s["gelu"], FB * t + HALF * (j + 1))
                    dve.tensor_copy(gT[:, b, 0, part], g[:, part]).then_inc(s["gh"], 1)
                    dve.wait_ge(s["gh"], 2 * t + (j + 1))
                    dve.tensor_tensor(gT[:, b, 1, part], g[:, part], gT[:, b, 0, part], ALU.subtract)\
                       .then_inc(s["gl"], 1)

            def result(t, b):
                e = expert(dve, t)
                dve.wait_ge(s["down"], t + 1)
                ge(dve, y_out[b], 8 * (t - b))
                dve.scalar_tensor_tensor(y[:, b], Y[b][:, :, :], 1 / W_SCALE,
                                         bias2[:, ds(e, 1), :].broadcast_to([P, RPT, D]), ALU.mult, ALU.add)\
                   .then_inc(s["y"], 1)
            tiles(dve.Fori, (split_gelu, 0), (split, 2), (result, -1))

        @block.tensor
        def _(pe):
            def transposes(t, b):
                pe.wait_ge(x_in[b], 8 * (t - b) + 16)
                ge(pe, s["xl"], t - 1)
                for h in range(DH):
                    for q in range(RPT):
                        mm = pe.transpose(T[b][:, h, q * P:(q + 1) * P], x[:, b, q, h * P:(h + 1) * P], ident[:, :])
                mm.then_inc(s["tr"], 1)

            def up(t, b):
                e = expert(pe, t)
                pe.wait_ge(lo[0], e + 1)
                pe.wait_ge(s["xl"], t + 1)
                for f in range(FB):
                    if f % FPB == 0:
                        ge(pe, s["gelu"], FB * (t - 1) + (f + FPB))
                    n = 0
                    for h in range(DH):
                        for wp, xps in ((0, (0, 1)), (1, (0,))):
                            wf = W1[:, wp, ds(e * DH + h, 1), f * P:(f + 1) * P].rearrange("p o f -> p (o f)")
                            for xp in xps:
                                mm = pe.matmul(Hb[f // FPB][:, f % FPB], wf, xT[:, b, xp, h], start=(n == 0),
                                               stop=(n == 3 * DH - 1))
                                n += 1
                    if f % FPB == FPB - 1:
                        mm.then_inc(s["up"], 1)

            def down(t, b):
                e = expert(pe, t)
                pe.wait_ge(lo[1], e + 1)
                ge(pe, s["y"], t - 1)
                pe.wait_ge(s["gl"], 2 * t + 2)
                for q in range(RPT):
                    n = 0
                    for f in range(FB):
                        for wp, gps in ((0, (0, 1)), (1, (0,))):
                            wf = W2[:, wp, ds(e * FB + f, 1), :].rearrange("p o d -> p (o d)")
                            for gp in gps:
                                mm = pe.matmul(Y[b][:, q], gT[:, b, gp, f, q * P:(q + 1) * P], wf, start=(n == 0),
                                               stop=(n == 3 * FB - 1))
                                n += 1
                mm.then_inc(s["down"], 1)
            tiles(pe.Fori, (up, 0), (transposes, 2), (down, -1))

        body.close()
        m.clear()


def final_phase(nc, ys_d, h_d, x1_d, place, weight, g2, b2, out):
    with ExitStack() as ctx:
        m = Memory(nc, ctx, "l")
        rows = m.sb("rows", [P, 2, D])
        ya = m.sb("ya", [P, 2, TPC, D])
        yb = m.sb("yb", [P, 2, TPC, D])
        h = m.sb("h", [P, 2, TPC, D])
        x1 = m.sb("x1", [P, 2, TPC, D])
        a = m.sb("a", [P, TPC, D])
        f = m.sb("f", [P, TPC, D])
        r = m.sb("r", [P, 2, TPC, D])
        res = m.sb("res", [P, 2, TPC, D])
        st = m.sb("st", [P, 2, TPC, 6])
        mv = m.sb("mv", [P, 2, TPC, 2])
        sm = m.sb("sm", [P, 7, TPC])
        s = {n: m.sem(n) for n in (
            "consts ga0 ga1 in0 in1 m1 m2 sta mva a1 sd1 a2 na fg fb stf mvf a3 sd2 a4 r res out0 out1 passed").split()}
        gathered = (s["ga0"], s["ga1"])
        loaded = (s["in0"], s["in1"])
        sent = (s["out0"], s["out1"])
        body = ctx.enter_context(ExitStack())
        block = body.enter_context(nc.Block())

        def chunks(fori, step):
            for c in range(2):
                step(c, c)
            with fori(1, CHUNKS // 2) as i:
                for b in range(2):
                    step(2 * i + b, b)

        def rows_of(d, c):
            return d.rearrange("(t p) d -> p t d", p=P)[:, ds(c * TPC, TPC), :]

        @block.sync
        def _(sp):
            sp.dma_start(rows[:, 0], g2.partition_broadcast(P)).then_inc(s["consts"], 16)
            sp.dma_start(rows[:, 1], b2.partition_broadcast(P)).then_inc(s["consts"], 16)

            def load(c, b):
                ge(sp, s["m1"], TPC * (c - 1))
                ge(sp, s["res"], c - 1)
                sp.dma_start(h[:, b], rows_of(h_d, c)).then_inc(loaded[b], 16)
                sp.dma_start(x1[:, b], rows_of(x1_d, c)).then_inc(loaded[b], 16)

            def store(c, b):
                sp.wait_ge(s["res"], c + 1)
                sp.dma_start(rows_of(out, c), res[:, b]).then_inc(sent[b], 16)
            load(0, 0)
            load(1, 1)
            store(0, 0)
            load(2, 0)
            store(1, 1)
            with sp.Fori(1, CHUNKS // 2 - 1) as i:
                for b in range(2):
                    load(2 * i + (1 + b), 1 - b)
                    store(2 * i + b, b)
            load(CHUNKS - 1, 1)
            store(CHUNKS - 2, 0)
            store(CHUNKS - 1, 1)
            for b in range(2):
                sp.wait_ge(sent[b], 8 * CHUNKS)

        @block.gpsimd
        def _(pool):
            for c in range(CHUNKS):
                for t in range(TPC):
                    ge(pool, s["m2"], TPC * (c - 2) + t + 1)
                    for k, y in enumerate((ya, yb)):
                        pool.indirect_dma_start(y[:, c % 2, t], None, ys_d, bass.IndirectOffsetOnAxis(
                            place[:, k, c * TPC + t:c * TPC + t + 1], 0)).then_inc(gathered[c % 2], 16)

        @block.scalar
        def _(act):
            def step(c, b):
                act.wait_ge(s["a1"], c + 1)
                act.activation(sm[:, 1], sm[:, 0], ACT.Sqrt).then_inc(s["sd1"], 1)
                act.wait_ge(s["a3"], c + 1)
                act.activation(sm[:, 4], sm[:, 3], ACT.Sqrt).then_inc(s["sd2"], 1)
                act.wait_ge(s["a4"], 2 * c + 2)
                ge(act, s["res"], c - 1)
                for t in range(TPC):
                    act.activation(r[:, b, t], f[:, t], ACT.Identity, bias=sm[:, 6, t:t + 1],
                                   scale=sm[:, 5, t:t + 1]).then_inc(s["r"], 1)
            chunks(act.Fori, step)

        @block.vector
        def _(dve):
            dve.wait_ge(s["consts"], 32)

            def step(c, b):
                dve.wait_ge(loaded[b], 16 * (c - b) + 32)
                dve.wait_ge(gathered[b], 64 * (c - b) + 128)
                for t in range(TPC):
                    wa = weight[:, 0, ds(c * TPC + t, 1)]
                    dve.scalar_tensor_tensor(ya[:, b, t], ya[:, b, t], wa, h[:, b, t], ALU.mult, ALU.add)\
                       .then_inc(s["m1"], 1)
                for t in range(TPC):
                    wb = weight[:, 1, ds(c * TPC + t, 1)]
                    dve.wait_ge(s["m1"], TPC * c + (t + 1))
                    dve.scalar_tensor_tensor(a[:, t], yb[:, b, t], wb, ya[:, b, t], ALU.mult, ALU.add)\
                       .then_inc(s["m2"], 1)
                for t in range(TPC):
                    dve.wait_ge(s["m2"], TPC * c + (t + 1))
                    dve.bn_stats(st[:, 0, t], a[:, t]).then_inc(s["sta"], 1)
                pause(dve, s["sta"], TPC * c + TPC, s["passed"])
                for t in range(TPC):
                    dve.bn_aggr(mv[:, 0, t], st[:, 0, t]).then_inc(s["mva"], 1)
                dve.wait_ge(s["mva"], TPC * c + TPC)
                dve.tensor_scalar(sm[:, 0], mv[:, 0, :, 1], LN_EPS, None, ALU.add).then_inc(s["a1"], 1)
                dve.wait_ge(s["sd1"], c + 1)
                dve.reciprocal(sm[:, 2], sm[:, 1]).then_inc(s["a2"], 1)
                dve.wait_ge(s["a2"], c + 1)
                for t in range(TPC):
                    dve.tensor_scalar(a[:, t], a[:, t], mv[:, 0, t, 0:1], sm[:, 2, t:t + 1], ALU.subtract, ALU.mult)\
                       .then_inc(s["na"], 1)
                dve.wait_ge(s["na"], TPC * c + TPC)
                dve.tensor_tensor(a[:, :, :], a[:, :, :], rows[:, 0].unsqueeze(1).broadcast_to([P, TPC, D]),
                                  ALU.mult).then_inc(s["fg"], 1)
                dve.wait_ge(s["fg"], c + 1)
                ge(dve, s["r"], TPC * c)
                dve.tensor_tensor(f[:, :, :], a[:, :, :], rows[:, 1].unsqueeze(1).broadcast_to([P, TPC, D]),
                                  ALU.add).then_inc(s["fb"], 1)
                dve.wait_ge(s["fb"], c + 1)
                for t in range(TPC):
                    dve.bn_stats(st[:, 1, t], f[:, t]).then_inc(s["stf"], 1)
                pause(dve, s["stf"], TPC * c + TPC, s["passed"])
                for t in range(TPC):
                    dve.bn_aggr(mv[:, 1, t], st[:, 1, t]).then_inc(s["mvf"], 1)
                dve.wait_ge(s["mvf"], TPC * c + TPC)
                dve.tensor_scalar(sm[:, 3], mv[:, 1, :, 1], LN_EPS, None, ALU.add).then_inc(s["a3"], 1)
                dve.wait_ge(s["sd2"], c + 1)
                dve.reciprocal(sm[:, 5], sm[:, 4]).then_inc(s["a4"], 1)
                dve.wait_ge(s["a4"], 2 * c + 1)
                dve.scalar_tensor_tensor(sm[:, 6], mv[:, 1, :, 0], -1.0, sm[:, 5], ALU.mult, ALU.mult)\
                   .then_inc(s["a4"], 1)
                dve.wait_ge(s["r"], TPC * c + TPC)
                ge(dve, sent[b], 8 * (c - b))
                dve.tensor_tensor(res[:, b], r[:, b], x1[:, b], ALU.add).then_inc(s["res"], 1)
            chunks(dve.Fori, step)

        body.close()
        m.clear()


def block_stack_kernel(nc, x, gate_w, gate_b, cand_w, cand_b, log_decay, out_wT, out_b, norm_w,
                       w_qkv, w_o, g1, b1, wg, w1, bb1, w2, bb2, g2, b2, out):
    def dram(name, shape, dt=F32):
        return nc.dram_tensor(name, shape, dt, kind="Internal").ap()

    x1_d, u2_d, h_d = (dram(n, [S, D]) for n in ("x1_d", "u2_d", "h_d"))
    qk_d = dram("qk_d", [3, 4, P, S], BF16)
    v_d = dram("v_d", [GROUPS, P, TILES, GROUP, HD + 1])
    oT_d = dram("oT_d", [HD + 1, HEADS, S])
    rz_d = dram("rz_d", [HEADS, S])
    places_d = dram("places_d", [TILE_SLOTS * PLACES, D])
    ys_d = dram("ys_d", [TILE_SLOTS * PLACES, D])
    with ExitStack() as ctx:
        m = Memory(nc, ctx, "k")
        ident = m.sb("ident", [P, P])
        place = m.sb("place", [P, 2, TILES], U32)
        weight = m.sb("weight", [P, 2, TILES])
        expert_of = m.sb("expert_of", [P, TILE_SLOTS], I32)
        front_phase(nc, ident, x, gate_w, gate_b, cand_w, cand_b, log_decay, out_wT, out_b, norm_w, w_qkv,
                    x1_d, u2_d, qk_d, v_d)
        attention_phase(nc, ident, qk_d, v_d, oT_d)
        route_phase(nc, ident, oT_d, rz_d, u2_d, w_o, g1, b1, wg, h_d, places_d, place, weight, expert_of)
        expert_phase(nc, ident, places_d, w1, bb1, w2, bb2, expert_of, ys_d)
        final_phase(nc, ys_d, h_d, x1_d, place, weight, g2, b2, out)


def kernel(**inputs):
    import numpy as np
    from concourse import bacc
    from concourse.bass_utils import run_bass_kernel_spmd

    a = {n.split("_", 2)[2]: np.asarray(v) for n, v in inputs.items()}

    def per_partition(v):
        return v.reshape(DH, P).T

    arrays = {
        "x": a["x"].reshape(S, D),
        "gate_w": a["gate_w"], "gate_b": per_partition(a["gate_b"]),
        "cand_w": a["cand_w"], "cand_b": per_partition(a["cand_b"]),
        "log_decay": per_partition(a["log_decay"]),
        "out_wT": a["out_w"].T, "out_b": a["out_b"], "norm_w": a["norm_w"], "w_qkv": a["w_qkv"],
        "w_o": a["w_o"].reshape(HEADS, HD, D).transpose(1, 0, 2).reshape(D, D),
        "g1": a["g1"], "b1": a["b1"], "wg": a["wg"], "w1": a["w1"],
        "bb1": a["bb1"].reshape(EXPERTS, FB, P).transpose(2, 0, 1).reshape(P, EXPERTS * FB),
        "w2": a["w2"], "bb2": a["bb2"], "g2": a["g2"], "b2": a["b2"],
    }
    nc = bacc.Bacc("TRN2", target_bir_lowering=False, num_devices=1)
    sent, args = {}, []
    for name, v in arrays.items():
        v = np.ascontiguousarray(v)
        sent[f"in_{name}"] = v
        args.append(nc.dram_tensor(f"in_{name}", v.shape, mybir.dt.from_np(v.dtype), kind="ExternalInput").ap())
    args.append(nc.dram_tensor("out", (S, D), F32, kind="ExternalOutput").ap())
    block_stack_kernel(nc, *args)
    r = run_bass_kernel_spmd(nc, [sent], core_ids=[0])
    return r.results[0]["out"].reshape(1, S, D)
```

```python
from contextlib import ExitStack

import concourse.bass as bass
from concourse import mybir

ALU = mybir.AluOpType
ACT = mybir.ActivationFunctionType
AX = mybir.AxisListType
F32 = mybir.dt.float32
F16 = mybir.dt.float16
BF16 = mybir.dt.bfloat16
U32 = mybir.dt.uint32
I32 = mybir.dt.int32

P = 128
S = 4096
D = 256
DH = D // P
TILES = S // P
CHUNK = 512
CHUNKS = S // CHUNK
TPC = CHUNK // P
TAPS = 7
PAD = TAPS // 2
HEADS = 16
HD = D // HEADS
GROUP = 4
GROUPS = HEADS // GROUP
EXPERTS = 8
F = 1024
FB = F // P
PLACES = 2 * P
RPT = PLACES // P
TILE_SLOTS = 2 * S // PLACES + EXPERTS
LN_EPS = 1e-5
RMS_EPS = 1.1920929e-07
MASKED = -1e30
ds = bass.ds


def ge(eng, sem, value):
    if not isinstance(value, int) or value > 0:
        eng.wait_ge(sem, value)


def pause(eng, sem, value, passed):
    eng.wait_ge(sem, value)
    eng.sem_inc(passed, 1)


class Memory:

    def __init__(self, nc, ctx, tag):
        self.nc, self.ctx, self.tag, self.sems = nc, ctx, tag, []

    def sb(self, name, shape, dt=F32):
        return self.ctx.enter_context(self.nc.sbuf_tensor(f"{self.tag}_{name}", shape, dt))

    def ps(self, name, shape=(P, CHUNK), dt=F32):
        return self.ctx.enter_context(self.nc.psum_tensor(f"{self.tag}_{name}", list(shape), dt))

    def sem(self, name):
        self.sems.append(self.ctx.enter_context(self.nc.semaphore(f"{self.tag}_{name}")))
        return self.sems[-1]

    def clear(self):
        with self.nc.Block() as block:
            @block.gpsimd
            def _(pool):
                for s in self.sems:
                    pool.sem_clear(s)


def expert_weights(w1, w2, e, k):
    return (w1[e].rearrange("(h p) f -> p h f", p=P), w2[e].rearrange("(k p) d -> p k d", p=P))[k]


def front_phase(nc, ident, x_in, gate_w, gate_b, cand_w, cand_b, log_decay, out_wT, out_b, norm_w, w_qkv,
                x1_d, u2_d, qk_d, v_d):
    with ExitStack() as ctx:
        m = Memory(nc, ctx, "f")
        X = m.sb("X", [P, TILES, D])
        UB = m.sb("UB", [P, TILES, D])
        uT = m.sb("uT", [P, DH, S + 2 * PAD])
        stats = m.sb("stats", [P, TILES, 6])
        mean = m.sb("mean", [P, TILES])
        rstd = m.sb("rstd", [P, TILES])
        tmp = m.sb("tmp", [P, 4, TILES])
        us = m.sb("us", [P, 2, TPC, D])
        taps = m.sb("taps", [P, 2, DH, TAPS])
        bias = m.sb("bias", [P, 2, DH])
        decay = m.sb("decay", [P, 2, DH])
        diag = m.sb("diag", [P, DH, TAPS, P])
        wout = m.sb("wout", [P, DH, D])
        wqkv = m.sb("wqkv", [P, DH, 3 * D])
        rows = m.sb("rows", [P, 2, D])
        tanh_g = m.sb("tanh_g", [P, 2, DH, CHUNK])
        cand = m.sb("cand", [P, DH, CHUNK])
        tanh_c = m.sb("tanh_c", [P, 2, DH, CHUNK])
        gated = m.sb("gated", [P, DH, CHUNK])
        hT = m.sb("hT", [P, 2, DH, CHUNK])
        y = m.sb("y", [P, TPC, D])
        junk = m.sb("junk", [P, D])
        ssq = m.sb("ssq", [P, TPC])
        z = m.sb("z", [P, TPC, D])
        r = m.sb("r", [P, TPC, D])
        x1 = m.sb("x1", [P, TPC, D])
        u2 = m.sb("u2", [P, TPC, D])
        st = m.sb("st", [P, 2, TPC, 6])
        mv = m.sb("mv", [P, 2, TPC, 2])
        sm = m.sb("sm", [P, 8, TPC])
        u2T = m.sb("u2T", [P, DH, CHUNK])
        rest = m.sb("rest", [P, 4, CHUNK])
        parts = m.sb("parts", [P, 3, 4, CHUNK], BF16)
        vt = m.sb("vt", [P, GROUPS, TPC, GROUP, HD + 1])
        G = [m.ps(f"G{h}") for h in range(DH)]
        Y = [m.ps(f"Y{h}") for h in range(2)]
        T = [m.ps(f"T{h}") for h in range(DH)]
        Q = [m.ps(f"Q{h}") for h in range(2)]

        s = {n: m.sem(n) for n in (
            "passed x_even x_odd consts ident0 ident1 exp_done diag_done ones stats1 mom var1 sd1 rstd1 us_done tr1 "
            "ut_done ub_done gate_conv tap tanh_g tanh_c gated scan proj y ssq z stz mvz a1 sdz a2 r x1 stx mvx "
            "a3 sdx a4 u2 tr2 u2T qk v hi res mid low vt x1_st u2_st qk_st v_st").split()}
        x_loaded = (s["x_even"], s["x_odd"])
        body = ctx.enter_context(ExitStack())
        block = body.enter_context(nc.Block())
        consts = [(taps[:, 0], gate_w.rearrange("(h p) o k -> p h (o k)", p=P)),
                  (taps[:, 1], cand_w.rearrange("(h p) o k -> p h (o k)", p=P)),
                  (bias[:, 0], gate_b),
                  (bias[:, 1], cand_b),
                  (decay[:, 0], log_decay),
                  (wout[:, :, :], out_wT.rearrange("(h p) e -> p h e", p=P)),
                  (wqkv[:, :, :], w_qkv.rearrange("(h p) e -> p h e", p=P)),
                  (rows[:, 0], out_b.partition_broadcast(P)),
                  (rows[:, 1], norm_w.partition_broadcast(P))]
        CONSTS = 16 * len(consts)

        def pipeline(fori, *pieces):
            def step(c, b):
                for work, lag in pieces:
                    if not isinstance(c, int):
                        work(c + lag, (b + lag) % 2)
                    elif 0 <= c + lag < CHUNKS:
                        work(c + lag, (b + lag) % 2)
            for c in range(-1, 3):
                step(c, c % 2)
            with fori(1, CHUNKS // 2 - 1) as i:
                for b in range(2):
                    step(2 * i + (1 + b), 1 - b)
            for c in range(CHUNKS - 1, CHUNKS + 2):
                step(c, c % 2)

        @block.sync
        def _(sp):
            xv = x_in.rearrange("(c t p) d -> c p t d", p=P, t=TPC)
            for c in range(CHUNKS):
                ge(sp, x_loaded[c % 2], 16 * (c // 2))
                sp.dma_start(X[:, c * TPC:(c + 1) * TPC, :], xv[c]).then_inc(x_loaded[c % 2], 16)

            def stage2(c, b):
                sp.wait_ge(s["x1"], TPC * c + TPC)
                sp.dma_start(x1_d.rearrange("(t p) d -> p t d", p=P)[:, ds(c * TPC, TPC), :], x1[:, :, :])\
                  .then_inc(s["x1_st"], 16)
                sp.wait_ge(s["u2"], c * TPC + TPC)
                sp.dma_start(u2_d.rearrange("(t p) d -> p t d", p=P)[:, ds(c * TPC, TPC), :], u2[:, :, :])\
                  .then_inc(s["u2_st"], 16)

            def stage3(c, b):
                sp.wait_ge(s["vt"], c * TPC + (TPC + 1))
                sp.dma_start(v_d.rearrange("g p t h d -> p g t (h d)")[:, :, ds(c * TPC, TPC), :],
                             vt[:, :, :, :, :].rearrange("p g t h d -> p g t (h d)")).then_inc(s["v_st"], 16)
                sp.wait_ge(s["hi"], 4 * c + 4)
                sp.wait_ge(s["mid"], 4 * c + 4)
                sp.wait_ge(s["low"], 4 * c + 4)
                sp.dma_start(qk_d.rearrange("s q p n -> p (s q) n")[:, :, ds(c * CHUNK, CHUNK)],
                             parts[:, :, :, :].rearrange("p s q n -> p (s q) n")).then_inc(s["qk_st"], 16)

            pipeline(sp.Fori, (stage3, -2), (stage2, -1))
            for n in ("x1_st", "u2_st", "v_st", "qk_st"):
                sp.wait_ge(s[n], 16 * CHUNKS)

        @block.gpsimd
        def _(pool):
            pool.memset(ident[:, :], 0.0).then_inc(s["ident0"], 1)
            for dst, src in consts:
                pool.dma_start(dst, src).then_inc(s["consts"], 16)
            pool.wait_ge(s["ident0"], 1)
            pool.affine_select(out=ident[:, :], in_=ident[:, :], compare_op=ALU.not_equal, fill=1.0, base=0,
                               pattern=[[-1, P]], channel_multiplier=1).then_inc(s["ident1"], 1)
            pool.memset(vt[:, :, :, :, HD:HD + 1], 1.0).then_inc(s["vt"], 1)
            pool.wait_ge(s["consts"], CONSTS)
            with pool.Fori(0, CHUNKS // 2) as i:
                for b in range(2):
                    pool.wait_ge(s["us_done"], (2 * i + b) * TPC + TPC)
                    pool.tensor_tensor(UB[:, ds((2 * i + b) * TPC, TPC), :], us[:, b],
                                       rows[:, 0].unsqueeze(1).broadcast_to([P, TPC, D]), ALU.add)\
                        .then_inc(s["ub_done"], 1)

            def low(c, b):
                ge(pool, s["qk_st"], 16 * c)
                for q in range(4):
                    pool.wait_ge(s["mid"], 4 * c + q + 1)
                    pool.tensor_tensor(parts[:, 2, q, :], rest[:, q, :], parts[:, 1, q, :], ALU.subtract)\
                        .then_inc(s["low"], 1)

            pipeline(pool.Fori, (low, -2))

        @block.scalar
        def _(act):
            act.wait_ge(s["consts"], CONSTS)
            act.activation(decay[:, 1], decay[:, 0], ACT.Exp).then_inc(s["exp_done"], 1)
            act.wait_ge(s["var1"], 1)
            act.activation(tmp[:, 3, :], tmp[:, 2, :], ACT.Sqrt).then_inc(s["sd1"], 1)
            act.mul(bias[:, 0], bias[:, 0], 0.5).then_inc(s["exp_done"], 1)
            with act.Fori(0, CHUNKS // 2) as i:
                for b in range(2):
                    for h in range(DH):
                        act.wait_ge(s["tr1"], i * (2 * DH) + (b * DH + h + 1))
                        act.copy(uT[:, h, ds(i * (2 * CHUNK) + (b * CHUNK + PAD), CHUNK)], (T, Q)[b][h][:, :])\
                           .then_inc(s["ut_done"], 1)
            act.wait_ge(s["exp_done"], 2)

            def tanhs(c, b):
                for h in range(DH):
                    act.wait_ge(s["tap"], (c + 1) * DH * TAPS)
                    ge(act, s["gated"], DH * (c - 1))
                    act.activation(tanh_c[:, b, h], cand[:, h], ACT.Tanh, bias=bias[:, 1, h:h + 1])\
                       .then_inc(s["tanh_c"], 1)
                for h in range(DH):
                    act.wait_ge(s["gate_conv"], c * DH + (h + 1))
                    ge(act, s["gated"], DH * (c - 1))
                    act.activation(tanh_g[:, b, h], G[h][:, :], ACT.Tanh, bias=bias[:, 0, h:h + 1], scale=0.5)\
                       .then_inc(s["tanh_g"], 1)

            def squares(c, b):
                act.wait_ge(s["y"], 2 * c + 2)
                for t in range(TPC):
                    if t:
                        act.wait_ge(s["ssq"], TPC * c + t)
                    else:
                        ge(act, s["ssq"], TPC * c)
                        ge(act, s["a1"], 2 * c)
                    act.activation(junk[:, :], y[:, t], ACT.Square, accum_out=ssq[:, t:t + 1])\
                       .then_inc(s["ssq"], 1)

            def normed(c, b):
                act.wait_ge(s["a1"], 2 * c + 2)
                act.activation(sm[:, 2, :], sm[:, 1, :], ACT.Sqrt).then_inc(s["sdz"], 1)
                act.wait_ge(s["a2"], 2 * c + 2)
                act.wait_ge(s["z"], 2 * c + 2)
                ge(act, s["x1"], TPC * c)
                for t in range(TPC):
                    act.activation(r[:, t], z[:, t], ACT.Identity, bias=sm[:, 4, t:t + 1],
                                   scale=sm[:, 3, t:t + 1]).then_inc(s["r"], 1)

            def deviation(c, b):
                act.wait_ge(s["a3"], c + 1)
                act.activation(sm[:, 6, :], sm[:, 5, :], ACT.Sqrt).then_inc(s["sdx"], 1)

            def turned(c, b):
                for h in range(DH):
                    act.wait_ge(s["tr2"], c * DH + (h + 1))
                    ge(act, s["v"], TPC * c)
                    act.copy(u2T[:, h], T[h][:, :]).then_inc(s["u2T"], 1)

            def high_middle(c, b):
                ge(act, s["qk_st"], 16 * c)
                for q in range(4):
                    act.wait_ge(s["qk"], 4 * c + q + 1)
                    act.copy(parts[:, 0, q], Q[q % 2][:, :]).then_inc(s["hi"], 1)
                    act.wait_ge(s["res"], 4 * c + q + 1)
                    act.copy(parts[:, 1, q], rest[:, q]).then_inc(s["mid"], 1)

            def v_out(c, b):
                ge(act, s["v_st"], 16 * c)
                for t in range(TPC):
                    act.wait_ge(s["v"], TPC * c + t + 1)
                    act.copy(vt[:, :, t, :, 0:HD], Q[t % 2][:, 0:D].rearrange("p (g h d) -> p g h d", g=GROUPS, h=GROUP))\
                       .then_inc(s["vt"], 1)

            pipeline(act.Fori, (tanhs, 0), (turned, -2), (high_middle, -2), (v_out, -2), (squares, -1), (normed, -1),
                     (deviation, -1))

        @block.vector
        def _(dve):
            dve.memset(uT[:, :, 0:PAD], 0.0).then_inc(s["ones"], 1)
            dve.memset(uT[:, :, S + PAD:S + 2 * PAD], 0.0).then_inc(s["ones"], 1)
            dve.memset(hT[:, 1, :, CHUNK - 1:CHUNK], 0.0).then_inc(s["ones"], 1)
            with dve.Fori(0, CHUNKS // 2) as i:
                for b in range(2):
                    dve.wait_ge(x_loaded[b], 16 * i + 16)
                    for t in range(TPC):
                        dve.bn_stats(stats[:, ds((2 * i + b) * TPC + t, 1), :].rearrange("p a b -> p (a b)"),
                                     X[:, ds((2 * i + b) * TPC + t, 1), :].rearrange("p a b -> p (a b)"))\
                           .then_inc(s["stats1"], 1)
            dve.wait_ge(s["consts"], CONSTS)
            dve.wait_ge(s["ident1"], 1)
            for h in range(DH):
                for k in range(TAPS):
                    dve.tensor_scalar(diag[:, h, k], ident[:, :], taps[:, 0, h, k:k + 1], None, ALU.mult)\
                       .then_inc(s["diag_done"], 1)
            dve.wait_ge(s["stats1"], TILES)
            me, mo = stats[:, :, 1], stats[:, :, 4]
            dve.tensor_tensor(tmp[:, 0], me, mo, ALU.add).then_inc(s["mom"], 1)
            dve.tensor_tensor(tmp[:, 1], me, mo, ALU.subtract).then_inc(s["mom"], 1)
            dve.tensor_tensor(tmp[:, 2], stats[:, :, 2], stats[:, :, 5], ALU.add).then_inc(s["mom"], 1)
            dve.wait_ge(s["mom"], 3)
            dve.tensor_scalar(mean[:, :], tmp[:, 0], 0.5, None, ALU.mult).then_inc(s["mom"], 1)
            dve.tensor_scalar(tmp[:, 2], tmp[:, 2], 1.0 / D, LN_EPS, ALU.mult, ALU.add).then_inc(s["mom"], 1)
            dve.scalar_tensor_tensor(tmp[:, 1], tmp[:, 1], 0.25, tmp[:, 1], ALU.mult, ALU.mult).then_inc(s["mom"], 1)
            dve.wait_ge(s["mom"], 6)
            dve.tensor_tensor(tmp[:, 2], tmp[:, 2], tmp[:, 1], ALU.add).then_inc(s["var1"], 1)
            dve.wait_ge(s["sd1"], 1)
            dve.reciprocal(rstd[:, :], tmp[:, 3, :]).then_inc(s["rstd1"], 1)
            dve.wait_ge(s["rstd1"], 1)

            def apply(c, i, b):
                for t in range(TPC):
                    if not isinstance(i, int):
                        dve.wait_ge(s["tr1"], DH * (c - 1))
                        dve.wait_ge(s["ub_done"], c - 1)
                    n = c * TPC + t
                    dve.tensor_scalar(us[:, b, t], X[:, ds(n, 1), :].rearrange("p a b -> p (a b)"),
                                      mean[:, ds(n, 1)], rstd[:, ds(n, 1)], ALU.subtract, ALU.mult)\
                       .then_inc(s["us_done"], 1)
            apply(0, 0, 0)
            apply(1, 0, 1)
            with dve.Fori(0, (CHUNKS - 2) // 2) as i:
                for b in range(2):
                    apply(2 * i + (2 + b), i + 1, b)
            dve.wait_ge(s["ut_done"], DH * CHUNKS)
            dve.wait_ge(s["ones"], 3)
            dve.wait_ge(s["exp_done"], 2)

            def conv(c, ks):
                for k in ks:
                    for h in range(DH):
                        n = k * DH + h
                        if k == 0:
                            ge(dve, s["tanh_c"], DH * c)
                            dve.tensor_scalar(cand[:, h], uT[:, h, ds(c * CHUNK, CHUNK)], taps[:, 1, h, 0:1],
                                              None, ALU.mult).then_inc(s["tap"], 1)
                        else:
                            dve.wait_ge(s["tap"], c * DH * TAPS + (n - DH + 1))
                            dve.scalar_tensor_tensor(cand[:, h], uT[:, h, ds(c * CHUNK + k, CHUNK)],
                                                     taps[:, 1, h, k:k + 1], cand[:, h], ALU.mult, ALU.add)\
                               .then_inc(s["tap"], 1)

            def taps_of(*ks):
                return lambda c, b: conv(c, ks)

            def scan(c, b):
                for h in range(DH):
                    dve.wait_ge(s["tanh_g"], DH * c + (h + 1))
                    dve.wait_ge(s["tanh_c"], DH * c + (h + 1))
                    ge(dve, s["scan"], DH * (c - 1) + (h + 1))
                    dve.scalar_tensor_tensor(gated[:, h], tanh_g[:, b, h], 1.0, tanh_c[:, b, h], ALU.add, ALU.mult)\
                       .then_inc(s["gated"], 1)
                for h in range(DH):
                    dve.wait_ge(s["gated"], DH * c + (h + 1))
                    if h == 0:
                        ge(dve, s["proj"], 2 * (c - 1))
                    dve.tensor_tensor_scan(out=hT[:, b, h], data0=decay[:, 1, h:h + 1].broadcast_to([P, CHUNK]),
                                           data1=gated[:, h], initial=hT[:, 1 - b, h, CHUNK - 1:CHUNK],
                                           op0=ALU.mult, op1=ALU.add).then_inc(s["scan"], 1)

            def branch(c, b):
                for j in range(2):
                    dve.wait_ge(s["proj"], 2 * c + j + 1)
                    ge(dve, s["ssq"], TPC * c)
                    dve.scalar_tensor_tensor(y[:, 2 * j:2 * j + 2].rearrange("p t d -> p (t d)"), Y[j][:, :], 0.5,
                                             UB[:, ds(c * TPC + 2 * j, 2), :].rearrange("p t d -> p (t d)"),
                                             ALU.mult, ALU.add).then_inc(s["y"], 1)
                for j in range(2):
                    dve.wait_ge(s["y"], 2 * c + j + 1)
                    ge(dve, s["r"], TPC * c)
                    dve.tensor_tensor(z[:, 2 * j:2 * j + 2], y[:, 2 * j:2 * j + 2],
                                      rows[:, 1].unsqueeze(1).broadcast_to([P, 2, D]), ALU.mult).then_inc(s["z"], 1)

            def moments(c, b):
                dve.wait_ge(s["z"], 2 * c + 2)
                for t in range(TPC):
                    dve.bn_stats(st[:, 0, t], z[:, t]).then_inc(s["stz"], 1)
                pause(dve, s["stz"], TPC * c + TPC, s["passed"])
                for t in range(TPC):
                    dve.bn_aggr(mv[:, 0, t], st[:, 0, t]).then_inc(s["mvz"], 1)

            def variance(c, b):
                dve.wait_ge(s["ssq"], TPC * c + TPC)
                dve.tensor_scalar(sm[:, 0], ssq[:, :], LN_EPS / D, LN_EPS * RMS_EPS, ALU.mult, ALU.add)\
                   .then_inc(s["a1"], 1)
                dve.wait_ge(s["a1"], 2 * c + 1)
                dve.wait_ge(s["mvz"], TPC * c + TPC)
                dve.tensor_tensor(sm[:, 1], sm[:, 0], mv[:, 0, :, 1], ALU.add).then_inc(s["a1"], 1)

            def scale(c, b):
                dve.wait_ge(s["sdz"], c + 1)
                dve.reciprocal(sm[:, 3], sm[:, 2]).then_inc(s["a2"], 1)
                dve.wait_ge(s["a2"], 2 * c + 1)
                dve.scalar_tensor_tensor(sm[:, 4], mv[:, 0, :, 0], -1.0, sm[:, 3], ALU.mult, ALU.mult)\
                   .then_inc(s["a2"], 1)

            def moments2(c, b):
                ge(dve, s["x1_st"], 16 * c)
                for t in range(TPC):
                    dve.wait_ge(s["r"], TPC * c + t + 1)
                    dve.tensor_tensor(x1[:, t], r[:, t], X[:, ds(c * TPC + t, 1), :].rearrange("p a b -> p (a b)"),
                                      ALU.add).then_inc(s["x1"], 1)
                for t in range(TPC):
                    dve.wait_ge(s["x1"], TPC * c + t + 1)
                    dve.bn_stats(st[:, 1, t], x1[:, t]).then_inc(s["stx"], 1)
                pause(dve, s["stx"], TPC * c + TPC, s["passed"])
                for t in range(TPC):
                    dve.bn_aggr(mv[:, 1, t], st[:, 1, t]).then_inc(s["mvx"], 1)
                dve.wait_ge(s["mvx"], TPC * c + TPC)
                dve.tensor_scalar(sm[:, 5], mv[:, 1, :, 1], LN_EPS, None, ALU.add).then_inc(s["a3"], 1)

            def norm2(c, b):
                dve.wait_ge(s["sdx"], c + 1)
                dve.reciprocal(sm[:, 7], sm[:, 6]).then_inc(s["a4"], 1)
                dve.wait_ge(s["a4"], c + 1)
                ge(dve, s["u2_st"], 16 * c)
                ge(dve, s["tr2"], DH * c)
                for t in range(TPC):
                    dve.tensor_scalar(u2[:, t], x1[:, t], mv[:, 1, t, 0:1], sm[:, 7, t:t + 1],
                                      ALU.subtract, ALU.mult).then_inc(s["u2"], 1)

            def residue(q):
                def work(c, b):
                    dve.wait_ge(s["hi"], 4 * c + q + 1)
                    ge(dve, s["low"], 4 * (c - 1) + q + 1)
                    dve.tensor_tensor(rest[:, q], Q[q % 2][:, :], parts[:, 0, q], ALU.subtract)\
                       .then_inc(s["res"], 1)
                return work

            pipeline(dve.Fori, (scan, 0), (residue(0), -2), (taps_of(0, 1), 1), (residue(1), -2), (taps_of(2), 1),
                     (residue(2), -2), (taps_of(3), 1), (residue(3), -2), (branch, -1), (taps_of(4), 1), (moments, -1),
                     (variance, -1), (taps_of(5), 1), (scale, -1), (taps_of(6), 1), (moments2, -1), (norm2, -1))

        @block.tensor
        def _(pe):
            pe.wait_ge(s["ident1"], 1)

            def transposes(c, src, waits, banks):
                for h in range(DH):
                    for t in range(TPC):
                        pe.wait_ge(waits, c * TPC + t + 1)
                        mm = pe.transpose(banks[h][:, t * P:(t + 1) * P], src(t, h), ident[:, :])
                    yield mm

            def transpose1(c, i, b):
                if not isinstance(i, int):
                    pe.wait_ge(s["ut_done"], DH * (c - 1))
                for mm in transposes(c, lambda t, h: us[:, b, t, h * P:(h + 1) * P], s["us_done"], (T, Q)[b]):
                    mm.then_inc(s["tr1"], 1)
            transpose1(0, 0, 0)
            transpose1(1, 0, 1)
            with pe.Fori(0, (CHUNKS - 2) // 2) as i:
                for b in range(2):
                    transpose1(2 * i + (2 + b), i + 1, b)
            pe.wait_ge(s["diag_done"], DH * TAPS)
            pe.wait_ge(s["ut_done"], DH * CHUNKS)
            pe.wait_ge(s["ones"], 3)
            pe.wait_ge(s["consts"], CONSTS)

            def stage1(c, b):
                for h in range(DH):
                    ge(pe, s["tanh_g"], DH * (c - 1) + (h + 1))
                    for k in range(TAPS):
                        mm = pe.matmul(G[h][:, :], diag[:, h, k], uT[:, h, ds(c * CHUNK + k, CHUNK)],
                                       start=(k == 0), stop=(k == TAPS - 1))
                    mm.then_inc(s["gate_conv"], 1)

            def stage2(c, b):
                pe.wait_ge(s["scan"], DH * c + DH)
                for j in range(2):
                    ge(pe, s["y"], 2 * (c - 1) + j + 1)
                    for t in (2 * j, 2 * j + 1):
                        for h in range(DH):
                            mm = pe.matmul(Y[j][:, (t % 2) * D:(t % 2 + 1) * D], hT[:, b, h, t * P:(t + 1) * P],
                                           wout[:, h, :], start=(h == 0), stop=(h == DH - 1))
                    mm.then_inc(s["proj"], 1)

            def stage2b(c, b):
                ge(pe, s["u2T"], DH * c)
                for mm in transposes(c, lambda t, h: u2[:, t, h * P:(h + 1) * P], s["u2"], T):
                    mm.then_inc(s["tr2"], 1)

            def stage3(c, b):
                pe.wait_ge(s["u2T"], DH * c + DH)
                ge(pe, s["vt"], TPC * c + 1)
                for q in range(4):
                    if q >= 2:
                        pe.wait_ge(s["res"], 4 * c + q - 1)
                    for h in range(DH):
                        mm = pe.matmul(Q[q % 2][:, :], wqkv[:, h, q * P:(q + 1) * P], u2T[:, h],
                                       start=(h == 0), stop=(h == DH - 1))
                    mm.then_inc(s["qk"], 1)
                for t in range(TPC):
                    if t < 2:
                        pe.wait_ge(s["res"], 4 * c + 3 + t)
                    else:
                        pe.wait_ge(s["vt"], TPC * c + t)
                    for h in range(DH):
                        mm = pe.matmul(Q[t % 2][:, 0:D], u2T[:, h, t * P:(t + 1) * P], wqkv[:, h, 2 * D:3 * D],
                                       start=(h == 0), stop=(h == DH - 1))
                    mm.then_inc(s["v"], 1)

            pipeline(pe.Fori, (stage1, 0), (stage2b, -2), (stage3, -2), (stage2, -1))

        body.close()
        m.clear()


K_PARTS = (0, 0, 0, 1, 1, 2)
Q_PARTS = (0, 1, 2, 0, 1, 0)
ROWS = HD * len(K_PARTS)
SHIFT = 2
VW = 32


def attention_phase(nc, qk_d, v_d, oT_d, places_d):
    BLOCKS = CHUNKS
    UNITS = BLOCKS * GROUPS
    LOAD = 16 * (2 * len(K_PARTS) + 1)
    IDX = GROUP * TPC

    diagonal = ([(3, (h,)) for h in range(GROUP)] + [(1, (0, 1)), (1, (2, 3))],
                [(2, (h,)) for h in range(GROUP)] + [(0, (0, 1)), (0, (2, 3))], [], [])
    DIAG_ITEMS = sum(len(d) for d in diagonal)

    ZERO_PIECES = RPT * TILE_SLOTS // 8
    TURN = 3

    def unit_follows(q, g):
        return not (isinstance(g, int) and (q, g) == (BLOCKS - 1, GROUPS - 1))

    def beside(q, g, kk, j):
        if not unit_follows(q, g):
            return []
        if kk is not None:
            return [(kk, j, (h,)) for h in range(GROUP)]
        more = {0: (0, 1), 1: (2,), 2: (3,)}.get(j, ()) if isinstance(g, int) else ()
        return [(q, t, (h,)) for t in more for h in range(GROUP)] + [(None, t, hs) for t, hs in diagonal[j]]

    STEP0, UNIT0 = 4, 2
    ITEM0 = DIAG_ITEMS
    def first_step(q, g):
        return g * (4 * (q + 1)) + (STEP0 + 4 * GROUPS * sum(range(1, q + 1)))

    def first_item(q, g):
        return g * (16 * q + DIAG_ITEMS) + \
            (ITEM0 + sum(GROUPS * (16 * b + DIAG_ITEMS) + 16 for b in range(q)))

    def unit(q, g):
        return g + (UNIT0 + GROUPS * q)

    def after(q, g):
        return (q + 1, 0) if isinstance(g, int) else (q, g + 1)

    def units(fori, work):
        for q in range(BLOCKS):
            with fori(0, GROUPS - 1) as g:
                work(q, g)
            work(q, GROUPS - 1)

    def walk(eng, q, g, step):
        e0, x0 = first_step(q, g), first_item(q, g)

        def four(kk, first, e, x):
            n = 0
            for j in range(4):
                items = beside(q, g, kk, j)
                step(kk, j, first and j == 0, e + j, x + n, items)
                n += len(items)
        if q:
            four(0, True, e0, x0)
        pairs = max(0, q - 1) // 2
        if pairs:
            with eng.Fori(0, pairs) as i:
                for k in (1, 2):
                    four(2 * i + k, False, i * 8 + (e0 + 4 * k), i * 32 + (x0 + 16 * k))
        if q > 1 + 2 * pairs:
            four(q - 1, False, e0 + 4 * (q - 1), x0 + 16 * (q - 1))
        four(None, q == 0, e0 + 4 * q, x0 + 16 * q)

    with ExitStack() as ctx:
        m = Memory(nc, ctx, "a")
        Kt = m.sb("K", [ROWS + SHIFT, GROUPS * GROUP * S], BF16)
        Qt = m.sb("Q", [ROWS + SHIFT, GROUPS * GROUP * CHUNK], BF16)
        Vg = m.sb("Vg", [P, GROUPS * TILES, GROUP * (HD + 1)])
        Vs = m.sb("Vs", [P, 4, GROUP, VW])
        Pt = m.sb("P", [P, 2, GROUP, CHUNK])
        identb = m.sb("identb", [P, P], BF16)
        mask_q = m.sb("mask_q", [P, P], BF16)
        mask_k = m.sb("mask_k", [P, P], BF16)
        ones = m.sb("ones", [P, P], BF16)
        mx = m.sb("mx", [P, BLOCKS * IDX])
        top = m.sb("top", [P, IDX])
        neg = m.sb("neg", [P, SHIFT, IDX], BF16)
        shift = m.sb("shift", [SHIFT * IDX, P], BF16)
        osb = m.sb("o", [P, CHUNK])
        zero = m.sb("zero", [P, D])
        ST = m.ps("ST", (P, GROUP, CHUNK))
        O = m.ps("O")
        M = [m.ps(f"M{b}") for b in range(2)]
        turned = m.ps("turned")

        s = {n: m.sem(n) for n in (
            "sp_passed pool_passed ones k_ones loaded setup ident st_a st_b exp_a exp_b pv vs item read top neg negT "
            "shift shift_sent o o_sent places").split()}
        st_ready = (s["st_a"], s["st_b"])
        exp_done = (s["exp_a"], s["exp_b"])
        body = ctx.enter_context(ExitStack())
        block = body.enter_context(nc.Block())

        def k_cols(g, h, col, width):
            return ds(g * (GROUP * S) + (h * S) + col, width)

        def q_cols(g, h, col, width):
            return ds(g * (GROUP * CHUNK) + (h * CHUNK + col), width)

        def unit_loaded(eng, q, g):
            eng.wait_ge(s["loaded"], g * LOAD + LOAD * (GROUPS * q + 1))

        @block.sync
        def _(sp):
            qk = qk_d.rearrange("s q p n -> s (q p) n")

            def load(q, g):
                for parts, to, at, row in ((Q_PARTS, Qt, q_cols(g, 0, 0, GROUP * CHUNK), 0),
                                           (K_PARTS, Kt, ds(g * (GROUP * S), GROUP * S), D)):
                    for b, part in enumerate(parts):
                        dst = to[b * HD:(b + 1) * HD, at].rearrange("d (h n) -> d h n", h=GROUP)
                        if to is Kt:
                            dst = dst[:, :, q * CHUNK:(q + 1) * CHUNK]
                        sp.dma_start(dst, qk[part, ds(g * (GROUP * HD) + row, GROUP * HD),
                                             q * CHUNK:(q + 1) * CHUNK].rearrange("(h d) n -> d h n", d=HD))\
                          .then_inc(s["loaded"], 16)
                sp.dma_start(Vg[:, ds(g * TILES + q * TPC, TPC), :],
                             v_d[ds(g, 1)].rearrange("o p t h d -> (o p) t (h d)")[:, q * TPC:(q + 1) * TPC])\
                  .then_inc(s["loaded"], 16)

            def send_shift(q, g):
                pause(sp, s["shift"], unit(q, g) + 1, s["sp_passed"])
                sp.dma_start(Qt[ROWS:ROWS + SHIFT, q_cols(g, 0, 0, GROUP * CHUNK)]
                             .rearrange("k (i q) -> k i q", i=IDX),
                             shift[:, :]).then_inc(s["shift_sent"], 16)

            for g in range(GROUPS):
                if g == 2:
                    send_shift(0, 0)
                if g == 1:
                    sp.wait_ge(s["ones"], 1)
                    for k in range(SHIFT):
                        for i in range(GROUPS):
                            sp.dma_start(Kt[ROWS + k:ROWS + k + 1, i * GROUP * S:(i + 1) * GROUP * S], ones[:, :])\
                              .then_inc(s["k_ones"], 16)
                if g:
                    unit_loaded(sp, 0, g - 1)
                load(0, g)

            def work(q, g):
                if unit_follows(q, g):
                    send_shift(*after(q, g))
                pause(sp, s["o"], unit(q, g) + 1, s["sp_passed"])
                for h in range(GROUP):
                    sp.dma_start(oT_d[:, ds(g * GROUP + h, 1), q * CHUNK:(q + 1) * CHUNK]
                                 .rearrange("d o n -> (d o) n"),
                                 osb[h * VW:h * VW + HD + 1, :]).then_inc(s["o_sent"], 16)
                if q + 1 < BLOCKS:
                    pause(sp, s["loaded"], g * LOAD + LOAD * (GROUPS * q + GROUPS), s["sp_passed"])
                    load(q + 1, g)
            units(sp.Fori, work)
            sp.wait_ge(s["o_sent"], 16 * GROUP * (UNITS + 1))
            sp.wait_ge(s["loaded"], LOAD * UNITS)
            sp.wait_ge(s["shift_sent"], 16 * (UNIT0 + UNITS))

        @block.gpsimd
        def _(pool):
            pool.memset(identb[:, :], 0.0).then_inc(s["ident"], 1)
            pool.memset(mask_q[:, :], 0.0).then_inc(s["ident"], 1)
            pool.memset(mask_k[:, :], 0.0).then_inc(s["ident"], 1)
            pool.memset(Vs[:, :, :, :], 0.0).then_inc(s["ident"], 1)
            pool.memset(zero[:, :], 0.0).then_inc(s["ident"], 1)
            pool.wait_ge(s["ident"], 5)
            pool.affine_select(out=identb[:, :], in_=identb[:, :], compare_op=ALU.not_equal, fill=1.0, base=0,
                               pattern=[[-1, P]], channel_multiplier=1).then_inc(s["setup"], 1)
            pool.affine_select(out=mask_q[:, :], in_=mask_q[:, :], compare_op=ALU.is_ge, fill=MASKED, base=0,
                               pattern=[[-1, P]], channel_multiplier=1).then_inc(s["setup"], 1)
            pool.affine_select(out=mask_k[:, :], in_=mask_k[:, :], compare_op=ALU.is_ge, fill=MASKED, base=0,
                               pattern=[[1, P]], channel_multiplier=-1).then_inc(s["setup"], 1)
            pool.sem_inc(s["vs"], STEP0)

            def work(q, g):
                pause(pool, s["loaded"], g * LOAD + LOAD * (GROUPS * q + 1), s["pool_passed"])

                def step(kk, j, first, e, x, items):
                    pause(pool, s["pv"], e - 3, s["pool_passed"])
                    at = q * TPC + j if kk is None else kk * TPC + j
                    pool.tensor_copy(Vs[:, j, :, 0:HD + 1], Vg[:, ds(g * TILES + at, 1), :]
                                     .rearrange("p o (h d) -> p (o h) d", h=GROUP)).then_inc(s["vs"], 1)
                walk(pool, q, g, step)
                if isinstance(g, int):
                    for k in range(ZERO_PIECES * q // BLOCKS, ZERO_PIECES * (q + 1) // BLOCKS):
                        pool.dma_start(places_d.rearrange("(t p) d -> p t d", p=P)[:, 8 * k:8 * k + 8, :],
                                       zero[:, :].unsqueeze(1).broadcast_to([P, 8, D])).then_inc(s["places"], 16)
            units(pool.Fori, work)
            pool.wait_ge(s["places"], 16 * ZERO_PIECES)

        @block.scalar
        def _(act):
            for e in exp_done:
                act.sem_inc(e, STEP0)
            act.sem_inc(s["o"], UNIT0)
            act.sem_inc(s["shift"], UNIT0)

            def take_shift(q, g):
                u = unit(q, g)
                act.wait_ge(s["negT"], u + 1)
                act.wait_ge(s["shift_sent"], 16 * u)
                act.copy(shift[:, :], turned[0:SHIFT * IDX, 0:P // 2].bitcast(BF16)).then_inc(s["shift"], 1)

            act.sem_inc(s["shift_sent"], 16 * UNIT0)
            take_shift(0, 0)

            def work(q, g):
                def step(kk, j, first, e, x, items):
                    c0 = j * P if kk is None else 0
                    if kk is None and j == TURN and unit_follows(q, g):
                        take_shift(*after(q, g))
                    act.wait_ge(s["pv"], e - 1)
                    for half in range(2):
                        hs = slice(2 * half, 2 * half + 2)
                        act.wait_ge(st_ready[half], e + 1)
                        act.activation(Pt[:, j % 2, hs, c0:], ST[:, hs, c0:], ACT.Exp, scale=HD ** -0.5)\
                           .then_inc(exp_done[half], 1)
                walk(act, q, g, step)
                act.wait_ge(s["pv"], first_step(*after(q, g)))
                act.wait_ge(s["o_sent"], unit(q, g) * (16 * GROUP) - 16 * GROUP * (UNIT0 - 1))
                act.copy(osb[:, :], O[:, :]).then_inc(s["o"], 1)
            units(act.Fori, work)

        @block.vector
        def _(dve):
            dve.memset(ones[:, :], 1.0).then_inc(s["ones"], 1)

            def read(item, b, x):
                kk, t, hs = item
                dve.wait_ge(s["item"], x + 1)
                width = CHUNK if kk is not None else (t + 1) * P
                at = (0 if kk is None else (kk + 1) * IDX) + (t * GROUP + hs[0])
                dve.tensor_reduce(mx[:, ds(at, len(hs))],
                                  M[b][:, 0:len(hs) * width].rearrange("p (h n) -> p h n", h=len(hs)),
                                  AX.X, ALU.max).then_inc(s["read"], 1)

            def finish(q, g, x):
                u = unit(q, g)
                dve.wait_ge(s["read"], x)
                dve.tensor_reduce(top[:, :].rearrange("p (h t) -> p t h", h=GROUP),
                                  mx[:, 0:(q + 1) * IDX].rearrange("p (k t h) -> p t h k", k=q + 1, t=TPC),
                                  AX.X, ALU.max).then_inc(s["top"], 1)
                dve.wait_ge(s["top"], u - UNIT0 + 1)
                if not (isinstance(u, int) and u == UNIT0):
                    dve.wait_ge(s["negT"], u)
                dve.tensor_scalar(neg[:, 0], top[:, :], -1.0, None, ALU.mult).then_inc(s["neg"], 1)
                dve.wait_ge(s["neg"], 2 * (u - UNIT0) + 1)
                dve.scalar_tensor_tensor(neg[:, 1], top[:, :], -1.0, neg[:, 0], ALU.mult, ALU.subtract)\
                   .then_inc(s["neg"], 1)

            x = 0
            for j in range(4):
                for t, hs in diagonal[j]:
                    read((None, t, hs), x % 2, x)
                    x += 1
            finish(0, 0, x)

            def work(q, g):
                def step(kk, j, first, e, x, items):
                    for i, item in enumerate(items):
                        if i == 0 and first:
                            dve.wait_ge(s["top"], unit(q, g) - UNIT0 + 1)
                        read(item, i % 2, x + i)
                walk(dve, q, g, step)
                if unit_follows(q, g):
                    finish(*after(q, g), first_item(*after(q, g)))
            units(dve.Fori, work)

        @block.tensor
        def _(pe):
            for e in (*st_ready, s["pv"]):
                pe.sem_inc(e, STEP0)
            pe.sem_inc(s["negT"], UNIT0)
            pe.sem_inc(s["o_sent"], 16 * GROUP)

            def scores(q, g, kk, j, e, half):
                c0 = j * P if kk is None else 0
                pe.wait_ge(exp_done[half], e)
                for h in (2 * half, 2 * half + 1):
                    keys = k_cols(g, h, (q if kk is None else kk) * CHUNK + j * P, P)
                    mm = pe.matmul(ST[:, h, c0:], Kt[:, keys], Qt[:, q_cols(g, h, c0, CHUNK - c0)],
                                   start=True, stop=kk is not None)
                    if kk is None:
                        mm = pe.matmul(ST[:, h, c0:c0 + P], identb[:, :], mask_k[:, :], start=False, stop=True)
                mm.then_inc(st_ready[half], 1)

            def values(diag, j, first, e, between=None):
                pe.wait_ge(exp_done[0], e + 1)
                pe.wait_ge(exp_done[1], e + 1)
                pe.wait_ge(s["vs"], e + 1)
                c0 = j * P if diag else 0
                cut = c0 if first or not between else max(c0, CHUNK // 2)
                for cols in (slice(c0, cut), slice(cut, CHUNK)):
                    if cols.start == cols.stop:
                        continue
                    for h in range(GROUP):
                        mm = pe.matmul(O[h * VW:(h + 1) * VW, cols], Vs[:, j, h], Pt[:, j % 2, h, cols],
                                       start=first, stop=True, skip_group_check=True)
                    if between and cols.stop < CHUNK:
                        between()
                        between = None
                mm.then_inc(s["pv"], 1)
                if between:
                    between()

            def item(q, g, what, b, x):
                kk, t, hs = what
                width = CHUNK if kk is not None else (t + 1) * P
                ge(pe, s["read"], x - 1)
                for i, h in enumerate(hs):
                    keys = k_cols(g, h, (q if kk is None else kk) * CHUNK, width)
                    mm = pe.matmul(M[b][:, i * width:(i + 1) * width], Qt[0:ROWS, q_cols(g, h, t * P, P)],
                                   Kt[0:ROWS, keys], start=True, stop=kk is not None)
                    if kk is None:
                        mm = pe.matmul(M[b][:, (i + 1) * width - P:(i + 1) * width], identb[:, :], mask_q[:, :],
                                       start=False, stop=True)
                mm.then_inc(s["item"], 1)

            def turn(u):
                pe.wait_ge(s["neg"], 2 * (u - UNIT0) + 2)
                if not isinstance(u, int) or u > UNIT0:
                    pe.wait_ge(s["shift"], u)
                pe.transpose(turned[0:SHIFT * IDX, 0:P // 2].bitcast(BF16),
                             neg[:, :, :].rearrange("p k i -> p (k i)"), identb[:, :]).then_inc(s["negT"], 1)

            pe.wait_ge(s["setup"], 3)
            unit_loaded(pe, 0, 0)
            x = 0
            for j in range(4):
                for t, hs in diagonal[j]:
                    item(0, 0, (None, t, hs), x % 2, x)
                    x += 1
            turn(UNIT0)
            pe.wait_ge(s["k_ones"], 16 * SHIFT * GROUPS)

            def work(q, g):
                u = unit(q, g)
                follows = unit_follows(q, g)
                if follows:
                    unit_loaded(pe, *after(q, g))

                def step(kk, j, first, e, x, items):
                    n = len(items)

                    def quarter(k):
                        for i in range(k * n // 4, (k + 1) * n // 4):
                            item(*after(q, g), items[i], i % 2, x + i)
                    if kk is None and j == TURN and follows:
                        turn(u + 1)
                    if first:
                        quarter(0)
                        quarter(1)
                        pe.wait_ge(s["shift_sent"], 16 * (u + 1))
                        scores(q, g, kk, j, e, 0)
                        scores(q, g, kk, j, e, 1)
                    else:
                        scores(q, g, kk, j, e, 0)
                        quarter(0)
                        scores(q, g, kk, j, e, 1)
                        quarter(1)
                    if first:
                        quarter(2)
                    else:
                        last_first = j == 1 and (q == 0 or isinstance(kk, int) and kk == 0)
                        if last_first:
                            pe.wait_ge(s["o"], u)
                        values(kk is None and j > 0, (j - 1) % 4, last_first, e - 1, (lambda: quarter(2)) if n else None)
                    quarter(3)
                walk(pe, q, g, step)
                values(True, 3, False, first_step(*after(q, g)) - 1)
            units(pe.Fori, work)

        body.close()
        m.clear()


def route_phase(nc, ident, oT_d, rz_d, u2_d, w_o, g1, b1, wg, w1, w2, h_d, places_d, place, weight, expert_of,
                stage):
    RZ_FIRST = 2
    COUNTED, ROUTED = 19, 37
    with ExitStack() as ctx:
        m = Memory(nc, ctx, "r")
        zs = m.sb("zs", [P, CHUNK])
        rz = m.sb("rz", [P, S])
        oT = m.sb("oT", [P, 2, DH, CHUNK])
        oN = m.sb("oN", [P, 2, DH, CHUNK])
        u2 = m.sb("u2", [P, 2, TPC, D])
        wo = m.sb("wo", [P, DH, D])
        wgs = m.sb("wg", [P, DH, EXPERTS])
        rows = m.sb("rows", [P, 2, D])
        a = m.sb("a", [P, TPC, D])
        hn = m.sb("hn", [P, TPC, D])
        hg = m.sb("hg", [P, TPC, D])
        hs = m.sb("h", [P, 2, TPC, D])
        H = m.sb("H", [P, TILES, D])
        hT = m.sb("hT", [P, DH, CHUNK])
        st = m.sb("st", [P, TPC, 6])
        mv = m.sb("mv", [P, TPC, 2])
        sm = m.sb("sm", [P, 3, TPC])
        L = m.sb("L", [P, TILES, EXPERTS])
        w = {n: m.sb(n, [P, TILES, EXPERTS]) for n in "e iota eq one1 one2 both pre t0 t1".split()}
        v = {n: m.sb(n, [P, TILES]) for n in "top1 top2 sum i1 i2 p1 p2".split()}
        tri = m.sb("tri", [P, P])
        one = m.sb("one", [P, P])
        cnt = m.sb("cnt", [P, EXPERTS])
        tot = m.sb("tot", [P, 6, EXPERTS])
        grid = m.sb("grid", [P, EXPERTS, TILES])
        gridc = m.sb("gridc", [P, EXPERTS, TILES])
        tl = m.sb("tl", [P, TILE_SLOTS, EXPERTS])
        tlc = m.sb("tlc", [P, TILE_SLOTS, EXPERTS])
        ef = m.sb("ef", [P, TILE_SLOTS])
        Y = [m.ps(f"Y{j}") for j in range(2)]
        T = [m.ps(f"T{h}") for h in range(DH)]
        G = m.ps("G")

        s = {n: m.sem(n) for n in (
            "passed z_in rz_done rz_out rz_in rz_rest in0 in1 consts oN proj a st mv a1 sd a2 hn hg h h_out0 h_out1 tr hT gate L setup "
            "rt exp pre pre_mm zero sent weights").split()}
        loaded = (s["in0"], s["in1"])
        h_out = (s["h_out0"], s["h_out1"])
        consts = [(wo[:, :, :], None), (wgs[:, :, :], wg.rearrange("(h p) e -> p h e", p=P)),
                  (rows[:, 0], g1.partition_broadcast(P)), (rows[:, 1], b1.partition_broadcast(P))]
        CONSTS = 16 * (len(consts))
        body = ctx.enter_context(ExitStack())
        block = body.enter_context(nc.Block())

        def chunks(fori, first, second):
            def pair(i):
                for b in range(2):
                    first(2 * i + (1 + b), 1 - b)
                    second(2 * i + b, b)
            first(0, 0)
            pair(0)
            with fori(1, CHUNKS // 2 - 1) as i:
                pair(i)
            first(CHUNKS - 1, 1)
            second(CHUNKS - 2, 0)
            second(CHUNKS - 1, 1)

        def nothing(c, b):
            pass

        @block.sync
        def _(sp):
            def load(c, b):
                ge(sp, s["a"], 2 * (c - 1))
                ge(sp, s["oN"], c - 1)
                for h in range(DH):
                    sp.dma_start(oT[:, b, h],
                                 oT_d[h * (HD // DH):(h + 1) * (HD // DH), :, ds(c * CHUNK, CHUNK)]
                                 .rearrange("d h n -> (d h) n")).then_inc(loaded[b], 16)
                sp.dma_start(u2[:, b], u2_d.rearrange("(t p) d -> p t d", p=P)[:, ds(c * TPC, TPC), :])\
                  .then_inc(loaded[b], 16)

            sp.dma_start(zs[:, :], oT_d[HD].rearrange("h (c n) -> (h c) n", n=CHUNK)).then_inc(s["z_in"], 16)
            sp.dma_start(wo[:, :, :], w_o.rearrange("(h p) e -> p h e", p=P)).then_inc(s["consts"], 16)
            for dst, src in consts[1:]:
                sp.dma_start(dst, src).then_inc(s["consts"], 16)
            sp.wait_ge(s["rz_done"], 1)
            sp.dma_start(rz_d.rearrange("h (c n) -> (h c) n", n=CHUNK), zs[:, :]).then_inc(s["rz_out"], 16)
            sp.wait_ge(s["rz_out"], 16)
            for cols, sem in ((slice(0, RZ_FIRST * CHUNK), s["rz_in"]), (slice(RZ_FIRST * CHUNK, S), s["rz_rest"])):
                sp.dma_start(rz[:, cols], rz_d[:, cols].partition_broadcast(P // HEADS)).then_inc(sem, 16)
                if sem is s["rz_in"]:
                    load(0, 0)
                    load(1, 1)

            with sp.Fori(1, CHUNKS // 2) as i:
                for b in range(2):
                    load(2 * i + b, b)
            for e in range(2):
                for k in range(2):
                    src = expert_weights(w1, w2, e, k)
                    sp.dma_start(stage[:, e, k].rearrange("p (a b) -> p a b", a=src.shape[1]), src)\
                      .then_inc(s["weights"], 16)
            sp.wait_ge(s["weights"], 64)

        @block.gpsimd
        def _(pool):
            pool.memset(tri[:, :], 1.0).then_inc(s["zero"], 1)
            pool.memset(one[:, :], 1.0).then_inc(s["setup"], 1)
            pool.wait_ge(s["zero"], 1)
            pool.affine_select(out=tri[:, :], in_=tri[:, :], compare_op=ALU.is_gt, fill=0.0, base=0,
                               pattern=[[1, P]], channel_multiplier=-1).then_inc(s["setup"], 1)
            for k, (t, pattern) in enumerate(((w["iota"], [[0, TILES], [1, EXPERTS]]),
                                              (grid, [[0, EXPERTS], [PLACES, TILES]]),
                                              (tl, [[1, TILE_SLOTS], [0, EXPERTS]]))):
                pool.iota(t[:, :, :], pattern=pattern, base=0, channel_multiplier=0,
                          allow_small_or_imprecise_dtypes=True).then_inc(s["setup"], 1)

            pool.wait_ge(s["rt"], ROUTED)
            pool.wait_ge(s["L"], 2 * CHUNKS)
            for t in range(TILES):
                for k in range(2):
                    pool.indirect_dma_start(places_d, bass.IndirectOffsetOnAxis(place[:, k, t:t + 1], 0), H[:, t],
                                            None).then_inc(s["sent"], 16)
            pool.wait_ge(s["sent"], 16 * 2 * TILES)

        @block.scalar
        def _(act):
            def second(c, b):
                act.wait_ge(s["a1"], c + 1)
                act.activation(sm[:, 1], sm[:, 0], ACT.Sqrt).then_inc(s["sd"], 1)
                for h in range(DH):
                    act.wait_ge(s["tr"], DH * c + (h + 1))
                    ge(act, s["gate"], TPC * c)
                    act.copy(hT[:, h], T[h][:, :]).then_inc(s["hT"], 1)
                act.wait_ge(s["h"], 2 * c + 2)
                act.dma_start(h_d.rearrange("(t p) d -> p t d", p=P)[:, ds(c * TPC, TPC), :], hs[:, b])\
                   .then_inc(h_out[b], 16)
                act.copy(H[:, ds(c * TPC, TPC), :], hs[:, b]).then_inc(s["L"], 1)
                act.wait_ge(s["gate"], TPC * c + TPC)
                act.copy(L[:, ds(c * TPC, TPC), :],
                         G[:, 0:TPC * EXPERTS].rearrange("p (t e) -> p t e", e=EXPERTS)).then_inc(s["L"], 1)
            chunks(act.Fori, nothing, second)
            for b in range(2):
                act.wait_ge(h_out[b], 16 * CHUNKS // 2)
            act.wait_ge(s["rt"], 2)
            act.activation(w["e"][:, :, :], w["e"][:, :, :], ACT.Exp).then_inc(s["exp"], 1)

        @block.vector
        def _(dve):
            dve.wait_ge(s["z_in"], 16)
            dve.reciprocal(zs[:, :], zs[:, :]).then_inc(s["rz_done"], 1)
            dve.wait_ge(s["rz_in"], 16)

            def first(c, b):
                dve.wait_ge(loaded[b], 24 * (c - b) + 48)
                ge(dve, s["proj"], 2 * (c - 1))
                if isinstance(c, int) and c == RZ_FIRST:
                    dve.wait_ge(s["rz_rest"], 16)
                dve.tensor_tensor(oN[:, b], oT[:, b],
                                  rz[:, ds(c * CHUNK, CHUNK)].unsqueeze(1).broadcast_to([P, DH, CHUNK]), ALU.mult)\
                   .then_inc(s["oN"], 1)

            def second(c, b):
                ge(dve, s["hn"], TPC * c)
                for j in range(2):
                    dve.wait_ge(s["proj"], 2 * c + (j + 1))
                    dve.tensor_tensor(a[:, 2 * j:2 * j + 2].rearrange("p t d -> p (t d)"), Y[j][:, :],
                                      u2[:, b, 2 * j:2 * j + 2].rearrange("p t d -> p (t d)"), ALU.add)\
                       .then_inc(s["a"], 1)
                for t in range(TPC):
                    if t % 2 == 0:
                        dve.wait_ge(s["a"], 2 * c + (t // 2 + 1))
                    dve.bn_stats(st[:, t], a[:, t]).then_inc(s["st"], 1)
                pause(dve, s["st"], TPC * c + TPC, s["passed"])
                for t in range(TPC):
                    dve.bn_aggr(mv[:, t], st[:, t]).then_inc(s["mv"], 1)
                dve.wait_ge(s["mv"], TPC * c + TPC)
                dve.tensor_scalar(sm[:, 0], mv[:, :, 1], LN_EPS, None, ALU.add).then_inc(s["a1"], 1)
                dve.wait_ge(s["sd"], c + 1)
                dve.reciprocal(sm[:, 2], sm[:, 1]).then_inc(s["a2"], 1)
                dve.wait_ge(s["a2"], c + 1)
                ge(dve, s["hg"], 2 * c)
                for t in range(TPC):
                    dve.tensor_scalar(hn[:, t], a[:, t], mv[:, t, 0:1], sm[:, 2, t:t + 1], ALU.subtract, ALU.mult)\
                       .then_inc(s["hn"], 1)
                for j in range(2):
                    half = slice(2 * j, 2 * j + 2)
                    dve.wait_ge(s["hn"], TPC * c + 2 * (j + 1))
                    dve.tensor_tensor(hg[:, half], hn[:, half], rows[:, 0].unsqueeze(1).broadcast_to([P, 2, D]),
                                      ALU.mult).then_inc(s["hg"], 1)
                ge(dve, h_out[b], 8 * (c - b))
                ge(dve, s["tr"], DH * (c - 1))
                ge(dve, s["L"], 2 * (c - 1))
                for j in range(2):
                    half = slice(2 * j, 2 * j + 2)
                    dve.wait_ge(s["hg"], 2 * c + (j + 1))
                    dve.tensor_tensor(hs[:, b, half], hg[:, half], rows[:, 1].unsqueeze(1).broadcast_to([P, 2, D]),
                                      ALU.add).then_inc(s["h"], 1)
            chunks(dve.Fori, first, second)

            n = [0]

            def did(ins):
                ins.then_inc(s["rt"], 1)
                n[0] += 1
                dve.wait_ge(s["rt"], n[0])

            def spread(x):
                return x.unsqueeze(2).broadcast_to([P, TILES, EXPERTS])
            dve.wait_ge(s["L"], 2 * CHUNKS)
            did(dve.tensor_reduce(v["top1"][:, :], L[:, :, :], AX.X, ALU.max))
            did(dve.tensor_tensor(w["e"][:, :, :], L[:, :, :], spread(v["top1"][:, :]), ALU.subtract))
            dve.wait_ge(s["exp"], 1)
            dve.wait_ge(s["setup"], 5)
            for k in (1, 2):
                top, i, one_hot = v[f"top{k}"], v[f"i{k}"], w[f"one{k}"]
                did(dve.tensor_reduce(top[:, :], w["e"][:, :, :], AX.X, ALU.max))
                did(dve.tensor_tensor(w["eq"][:, :, :], w["e"][:, :, :], spread(top[:, :]), ALU.is_lt))
                did(dve.scalar_tensor_tensor(w["eq"][:, :, :], w["eq"][:, :, :], float(EXPERTS),
                                             w["iota"][:, :, :], ALU.mult, ALU.add))
                did(dve.tensor_reduce(i[:, :], w["eq"][:, :, :], AX.X, ALU.min))
                did(dve.tensor_tensor(one_hot[:, :, :], w["iota"][:, :, :], spread(i[:, :]), ALU.is_equal))
                if k == 1:
                    did(dve.scalar_tensor_tensor(w["e"][:, :, :], one_hot[:, :, :], -2.0, w["e"][:, :, :],
                                                 ALU.mult, ALU.add))
            did(dve.tensor_tensor(v["sum"][:, :], v["top1"][:, :], v["top2"][:, :], ALU.add))
            did(dve.reciprocal(v["sum"][:, :], v["sum"][:, :]))
            did(dve.tensor_tensor(weight[:, 0], v["top1"][:, :], v["sum"][:, :], ALU.mult))
            did(dve.tensor_tensor(weight[:, 1], v["top2"][:, :], v["sum"][:, :], ALU.mult))
            did(dve.tensor_tensor(w["both"][:, :, :], w["one1"][:, :, :], w["one2"][:, :, :], ALU.add))
            for e in range(EXPERTS):
                scan = dve.tensor_tensor_scan(out=w["pre"][:, :, e], data0=one[:, 0:TILES],
                                              data1=w["both"][:, :, e], initial=0.0, op0=ALU.mult, op1=ALU.add)
                scan.then_inc(s["pre"], 1)
            dve.wait_ge(s["pre"], EXPERTS)
            did(dve.tensor_copy(cnt[:, :], w["pre"][:, TILES - 1, :]))
            dve.wait_ge(s["pre_mm"], 1)
            did(dve.tensor_copy(tot[:, 0], G[:, 0:EXPERTS]))
            did(dve.tensor_copy(tot[:, 1], G[:, EXPERTS:2 * EXPERTS]))
            did(dve.tensor_tensor(gridc[:, :, :], grid[:, :, :],
                                  tot[:, 1].unsqueeze(2).broadcast_to([P, EXPERTS, TILES]), ALU.is_lt))
            did(dve.tensor_reduce(tot[:, 2], gridc[:, :, :], AX.X, ALU.add))
            did(dve.tensor_tensor_scan(out=tot[:, 3], data0=one[:, 0:EXPERTS], data1=tot[:, 2], initial=0.0,
                                       op0=ALU.mult, op1=ALU.add))
            did(dve.tensor_tensor(tot[:, 4], tot[:, 3], tot[:, 2], ALU.subtract))
            did(dve.scalar_tensor_tensor(tot[:, 5], tot[:, 4], float(PLACES), tot[:, 0], ALU.mult, ALU.add))
            did(dve.tensor_tensor(w["t0"][:, :, :], w["pre"][:, :, :], w["both"][:, :, :], ALU.subtract))
            did(dve.tensor_tensor(w["t1"][:, :, :], w["t0"][:, :, :],
                                  tot[:, 5].unsqueeze(1).broadcast_to([P, TILES, EXPERTS]), ALU.add))
            for k in (1, 2):
                did(dve.tensor_tensor(w["t0"][:, :, :], w["t1"][:, :, :], w[f"one{k}"][:, :, :], ALU.mult))
                did(dve.tensor_reduce(v[f"p{k}"][:, :], w["t0"][:, :, :], AX.X, ALU.add))
                did(dve.tensor_copy(place[:, k - 1], v[f"p{k}"][:, :]))
            did(dve.tensor_tensor(tlc[:, :, :], tl[:, :, :],
                                  tot[:, 3].unsqueeze(1).broadcast_to([P, TILE_SLOTS, EXPERTS]), ALU.is_ge))
            did(dve.tensor_reduce(ef[:, :], tlc[:, :, :], AX.X, ALU.add))
            did(dve.tensor_scalar(expert_of[:, :], ef[:, :], float(EXPERTS - 1), None, ALU.min))
            assert n[0] == ROUTED, n

        @block.tensor
        def _(pe):
            pe.wait_ge(s["consts"], CONSTS)

            def first(c, b):
                pe.wait_ge(s["oN"], c + 1)
                for j in range(2):
                    ge(pe, s["a"], 2 * (c - 1) + (j + 1))
                    for t in (2 * j, 2 * j + 1):
                        for h in range(DH):
                            mm = pe.matmul(Y[j][:, (t % 2) * D:(t % 2 + 1) * D], oN[:, b, h, t * P:(t + 1) * P],
                                           wo[:, h, :], start=(h == 0), stop=(h == DH - 1))
                    mm.then_inc(s["proj"], 1)

            def second(c, b):
                pe.wait_ge(s["h"], 2 * c + 2)
                ge(pe, s["hT"], DH * c)
                for h in range(DH):
                    for t in range(TPC):
                        mm = pe.transpose(T[h][:, t * P:(t + 1) * P], hs[:, b, t, h * P:(h + 1) * P], ident[:, :])
                    mm.then_inc(s["tr"], 1)
                pe.wait_ge(s["hT"], DH * c + DH)
                ge(pe, s["L"], 2 * c)
                for t in range(TPC):
                    for h in range(DH):
                        mm = pe.matmul(G[:, t * EXPERTS:(t + 1) * EXPERTS], hT[:, h, t * P:(t + 1) * P], wgs[:, h, :],
                                       start=(h == 0), stop=(h == DH - 1))
                    mm.then_inc(s["gate"], 1)
            chunks(pe.Fori, first, second)
            pe.wait_ge(s["setup"], 5)
            pe.wait_ge(s["rt"], COUNTED)
            pe.matmul(G[:, 0:EXPERTS], tri[:, :], cnt[:, :], start=True, stop=True)
            pe.matmul(G[:, EXPERTS:2 * EXPERTS], one[:, :], cnt[:, :], start=True, stop=True).then_inc(s["pre_mm"], 1)

        body.close()
        m.clear()


W_SCALE = 64.0


def expert_phase(nc, ident, stage, places_d, w1, bb1, w2, bb2, expert_of, ys_d):
    AHEAD = 4
    BANKS = 4
    FPB = FB // BANKS
    HALF = FB // 2
    with ExitStack() as ctx:
        m = Memory(nc, ctx, "e")
        W1 = m.sb("W1", [P, 2, EXPERTS * DH, F], F16)
        W2 = m.sb("W2", [P, 2, EXPERTS * FB, D], F16)
        bias1 = m.sb("bias1", [P, EXPERTS * FB])
        bias2 = m.sb("bias2", [P, EXPERTS, D])
        x = m.sb("x", [P, 2, RPT, D])
        xT = m.sb("xT", [P, 2, 2, DH, PLACES], F16)
        g = m.sb("g", [P, FB, PLACES])
        gT = m.sb("gT", [P, 2, 2, FB, PLACES], F16)
        y = m.sb("y", [P, 2, RPT, D])
        T = [m.ps(f"T{b}", (P, DH, PLACES)) for b in range(2)]
        Hb = [m.ps(f"H{k}", (P, FPB, PLACES)) for k in range(BANKS)]
        Y = [m.ps(f"Y{b}", (P, RPT, D)) for b in range(2)]

        s = {n: m.sem(n) for n in (
            "consts v00 v01 v10 v11 sc1 sc2 hi1 hi2 lo1 lo2 x0 x1 tr xh xl up gelu gh gl down y y_out0 y_out1").split()}
        loaded = ((s["v00"], s["v01"]), (s["v10"], s["v11"]))
        x_in = (s["x0"], s["x1"])
        y_out = (s["y_out0"], s["y_out1"])
        scaled, hi, lo = ((s[f"{n}1"], s[f"{n}2"]) for n in ("sc", "hi", "lo"))
        body = ctx.enter_context(ExitStack())
        block = body.enter_context(nc.Block())

        def tiles(fori, *stages):
            def step(t, b):
                for work, lag in stages:
                    if not isinstance(t, int):
                        work(t + lag, (b + lag) % 2)
                    elif 0 <= t + lag < TILE_SLOTS:
                        work(t + lag, (b + lag) % 2)
            for t in range(-AHEAD, 3):
                step(t, t % 2)
            with fori(1, (TILE_SLOTS - AHEAD) // 2 - 1) as i:
                for b in range(2):
                    step(2 * i + (1 + b), 1 - b)
            for t in range(TILE_SLOTS - AHEAD - 1, TILE_SLOTS + 1):
                step(t, t % 2)

        def expert(eng, t):
            return eng.value_load(expert_of[0:1, ds(t, 1)], min_val=0, max_val=EXPERTS - 1)

        def weights(e, k):
            W, n = ((W1, DH), (W2, FB))[k]
            return (stage[:, e % 2, k].rearrange("p (a b) -> p a b", a=n),
                    W[:, 0, e * n:(e + 1) * n, :], W[:, 1, e * n:(e + 1) * n, :])

        @block.sync
        def _(sp):
            def load(t, b):
                ge(sp, s["tr"], t - 1)
                sp.dma_start(x[:, b], places_d[ds(t * PLACES, PLACES), :].rearrange("(q p) d -> p q d", p=P))\
                  .then_inc(x_in[b], 16)
                if isinstance(t, int) and t == 1:
                    sp.dma_start(bias1[:, :], bb1).then_inc(s["consts"], 16)
                    sp.dma_start(bias2[:, :, :], bb2.partition_broadcast(P)).then_inc(s["consts"], 16)

            def store(t, b):
                sp.wait_ge(s["y"], t + 1)
                sp.dma_start(ys_d[ds(t * PLACES, PLACES), :].rearrange("(q p) d -> p q d", p=P), y[:, b])\
                  .then_inc(y_out[b], 16)
            tiles(sp.Fori, (load, AHEAD), (store, -1))
            for b in range(2):
                sp.wait_ge(y_out[b], 8 * TILE_SLOTS)

        def split_on_pool(pool, e, k):
            whole, high, low = weights(e, k)
            pool.wait_ge(loaded[e % 2][k], 16 * (e // 2))
            pool.tensor_scalar(whole, whole, W_SCALE, None, ALU.mult).then_inc(scaled[k], 1)
            pool.wait_ge(scaled[k], e - 1)
            pool.tensor_copy(high, whole).then_inc(hi[k], 1)
            pool.wait_ge(hi[k], e + 1)
            pool.wait_ge(lo[k], e)
            pool.tensor_tensor(low, whole, high, ALU.subtract).then_inc(lo[k], 1)

        @block.gpsimd
        def _(pool):
            for e in range(2, EXPERTS):
                for k in range(2):
                    pool.wait_ge(lo[k], e - 1)
                    pool.dma_start(weights(e, k)[0], expert_weights(w1, w2, e, k)).then_inc(loaded[e % 2][k], 16)
                if e == 2:
                    continue
                for k in range(2):
                    split_on_pool(pool, e - 1, k)
            for k in range(2):
                split_on_pool(pool, EXPERTS - 1, k)

        @block.scalar
        def _(act):
            def high_parts(e):
                for k in range(2):
                    whole, high, low = weights(e, k)
                    act.activation(high, whole, ACT.Copy, scale=W_SCALE).then_inc(hi[k], 1)

            def split(t, b):
                act.wait_ge(s["tr"], t + 1)
                ge(act, s["up"], BANKS * (t - 1))
                act.copy(xT[:, b, 0], T[b][:, :, :]).then_inc(s["xh"], 1)
                if isinstance(t, int) and t == 1:
                    high_parts(1)

            def gelu(t, b):
                e = expert(act, t)
                for f in range(FB):
                    if f % FPB == 0:
                        act.wait_ge(s["up"], BANKS * t + (f // FPB + 1))
                    if f % HALF == 0:
                        ge(act, s["gl"], 2 * (t - 1) + (f // HALF + 1))
                    act.activation(g[:, f], Hb[f // FPB][:, f % FPB], ACT.Gelu_apprx_tanh,
                                   bias=bias1[:, ds(e * FB + f, 1)], scale=1 / W_SCALE).then_inc(s["gelu"], 1)
            high_parts(0)
            act.wait_ge(s["consts"], 32)
            tiles(act.Fori, (gelu, 0), (split, 2))

        @block.vector
        def _(dve):
            def low_parts(e):
                for k in range(2):
                    whole, high, low = weights(e, k)
                    dve.wait_ge(hi[k], e + 1)
                    dve.scalar_tensor_tensor(low, whole, W_SCALE, high, ALU.mult, ALU.subtract).then_inc(lo[k], 1)

            def split(t, b):
                dve.wait_ge(s["xh"], t + 1)
                dve.tensor_tensor(xT[:, b, 1], T[b][:, :, :], xT[:, b, 0], ALU.subtract).then_inc(s["xl"], 1)
                if isinstance(t, int) and t == 1:
                    low_parts(1)

            def split_gelu(t, b):
                ge(dve, s["down"], t - 1)
                for j in range(2):
                    part = slice(j * HALF, (j + 1) * HALF)
                    dve.wait_ge(s["gelu"], FB * t + HALF * (j + 1))
                    dve.tensor_copy(gT[:, b, 0, part], g[:, part]).then_inc(s["gh"], 1)
                    dve.wait_ge(s["gh"], 2 * t + (j + 1))
                    dve.tensor_tensor(gT[:, b, 1, part], g[:, part], gT[:, b, 0, part], ALU.subtract)\
                       .then_inc(s["gl"], 1)

            def result(t, b):
                e = expert(dve, t)
                dve.wait_ge(s["down"], t + 1)
                ge(dve, y_out[b], 8 * (t - b))
                dve.scalar_tensor_tensor(y[:, b], Y[b][:, :, :], 1 / W_SCALE,
                                         bias2[:, ds(e, 1), :].broadcast_to([P, RPT, D]), ALU.mult, ALU.add)\
                   .then_inc(s["y"], 1)
            low_parts(0)
            dve.wait_ge(s["consts"], 32)
            tiles(dve.Fori, (split_gelu, 0), (split, 2), (result, -1))

        @block.tensor
        def _(pe):
            def transposes(t, b):
                pe.wait_ge(x_in[b], 8 * (t - b) + 16)
                ge(pe, s["xl"], t - 1)
                for h in range(DH):
                    for q in range(RPT):
                        mm = pe.transpose(T[b][:, h, q * P:(q + 1) * P], x[:, b, q, h * P:(h + 1) * P], ident[:, :])
                mm.then_inc(s["tr"], 1)

            def up(t, b):
                e = expert(pe, t)
                pe.wait_ge(lo[0], e + 1)
                pe.wait_ge(s["xl"], t + 1)
                for f in range(FB):
                    if f % FPB == 0:
                        ge(pe, s["gelu"], FB * (t - 1) + (f + FPB))
                    n = 0
                    for h in range(DH):
                        for wp, xps in ((0, (0, 1)), (1, (0,))):
                            wf = W1[:, wp, ds(e * DH + h, 1), f * P:(f + 1) * P].rearrange("p o f -> p (o f)")
                            for xp in xps:
                                mm = pe.matmul(Hb[f // FPB][:, f % FPB], wf, xT[:, b, xp, h], start=(n == 0),
                                               stop=(n == 3 * DH - 1))
                                n += 1
                    if f % FPB == FPB - 1:
                        mm.then_inc(s["up"], 1)

            def down(t, b):
                e = expert(pe, t)
                pe.wait_ge(lo[1], e + 1)
                ge(pe, s["y"], t - 1)
                pe.wait_ge(s["gl"], 2 * t + 2)
                for q in range(RPT):
                    n = 0
                    for f in range(FB):
                        for wp, gps in ((0, (0, 1)), (1, (0,))):
                            wf = W2[:, wp, ds(e * FB + f, 1), :].rearrange("p o d -> p (o d)")
                            for gp in gps:
                                mm = pe.matmul(Y[b][:, q], gT[:, b, gp, f, q * P:(q + 1) * P], wf, start=(n == 0),
                                               stop=(n == 3 * FB - 1))
                                n += 1
                mm.then_inc(s["down"], 1)
            tiles(pe.Fori, (up, 0), (transposes, 2), (down, -1))

        body.close()
        m.clear()


def final_phase(nc, ys_d, h_d, x1_d, place, weight, g2, b2, out):
    with ExitStack() as ctx:
        m = Memory(nc, ctx, "l")
        rows = m.sb("rows", [P, 2, D])
        ya = m.sb("ya", [P, TILES, D])
        yb = m.sb("yb", [P, TILES, D])
        h = m.sb("h", [P, TILES, D])
        x1 = m.sb("x1", [P, TILES, D])
        a = m.sb("a", [P, 2, TPC, D])
        f = m.sb("f", [P, 2, TPC, D])
        st = m.sb("st", [P, 2, TPC, 6])
        mv = m.sb("mv", [P, 2, TPC, 2])
        na = m.sb("na", [P, TPC, D])
        g = m.sb("g", [P, TPC, D])
        sm = m.sb("sm", [P, 8, TPC])
        s = {n: m.sem(n) for n in (
            "consts ga0 ga1 in0 in1 m1 m2 sta mva a1 sd1 a2 na fg fb stf mvf a3 sd2 a4 r res sent passed").split()}
        gathered = (s["ga0"], s["ga1"])
        loaded = (s["in0"], s["in1"])
        body = ctx.enter_context(ExitStack())
        block = body.enter_context(nc.Block())

        def chunks(fori, *pieces):
            def step(c, b):
                for work, lag in pieces:
                    if not isinstance(c, int) or 0 <= c + lag < CHUNKS:
                        work(c + lag, (b + lag) % 2)
            for c in range(-1, 3):
                step(c, c % 2)
            with fori(1, CHUNKS // 2 - 1) as i:
                for b in range(2):
                    step(2 * i + (1 + b), 1 - b)
            step(CHUNKS - 1, 1)

        def rows_of(d, c):
            return d.rearrange("(t p) d -> p t d", p=P)[:, ds(c * TPC, TPC), :]

        def tiles_of(x, c):
            return x[:, ds(c * TPC, TPC), :]

        def tile_of(x, c, t):
            return x[:, ds(c * TPC + t, 1), :].rearrange("p o d -> p (o d)")

        @block.sync
        def _(sp):
            sp.dma_start(rows[:, 0], g2.partition_broadcast(P)).then_inc(s["consts"], 16)
            sp.dma_start(rows[:, 1], b2.partition_broadcast(P)).then_inc(s["consts"], 16)
            for c in range(CHUNKS):
                ge(sp, loaded[c % 2], 32 * (c // 2))
                sp.dma_start(tiles_of(h, c), rows_of(h_d, c)).then_inc(loaded[c % 2], 16)
                sp.dma_start(tiles_of(x1, c), rows_of(x1_d, c)).then_inc(loaded[c % 2], 16)

            def store(c, b):
                sp.wait_ge(s["res"], c + 1)
                sp.dma_start(rows_of(out, c), tiles_of(x1, c)).then_inc(s["sent"], 16)
            chunks(sp.Fori, (store, 0))
            sp.wait_ge(s["sent"], 16 * CHUNKS)

        @block.gpsimd
        def _(pool):
            for c in range(CHUNKS):
                ge(pool, gathered[c % 2], 16 * 2 * TPC * (c // 2))
                for t in range(c * TPC, (c + 1) * TPC):
                    for k, y in enumerate((ya, yb)):
                        pool.indirect_dma_start(y[:, t], None, ys_d, bass.IndirectOffsetOnAxis(
                            place[:, k, t:t + 1], 0)).then_inc(gathered[c % 2], 16)

            def result(c, b):
                pool.wait_ge(s["r"], TPC * c + TPC)
                pool.tensor_tensor(tiles_of(x1, c), tiles_of(ya, c), tiles_of(x1, c), ALU.add)\
                    .then_inc(s["res"], 1)
            for b in range(2):
                pool.wait_ge(loaded[b], 32 * CHUNKS // 2)
            chunks(pool.Fori, (result, 0))

        @block.scalar
        def _(act):
            def deviation1(c, b):
                act.wait_ge(s["a1"], c + 1)
                act.activation(sm[:, 1], sm[:, 0], ACT.Sqrt).then_inc(s["sd1"], 1)

            def normed1(c, b):
                act.wait_ge(s["a2"], 2 * c + 2)
                ge(act, s["fg"], 2 * c)
                for t in range(TPC):
                    act.activation(na[:, t], a[:, b, t], ACT.Identity, bias=sm[:, 7, t:t + 1],
                                   scale=sm[:, 2, t:t + 1]).then_inc(s["na"], 1)

            def deviation2(c, b):
                act.wait_ge(s["a3"], c + 1)
                act.activation(sm[:, 4], sm[:, 3], ACT.Sqrt).then_inc(s["sd2"], 1)

            def normed(c, b):
                act.wait_ge(s["a4"], 2 * c + 2)
                for t in range(TPC):
                    act.activation(tile_of(ya, c, t), f[:, b, t], ACT.Identity, bias=sm[:, 6, t:t + 1],
                                   scale=sm[:, 5, t:t + 1]).then_inc(s["r"], 1)
            chunks(act.Fori, (normed1, 0), (deviation2, 0), (deviation1, 1), (normed, 0))

        @block.vector
        def _(dve):
            dve.wait_ge(s["consts"], 32)

            def gather(c, b):
                ge(dve, s["na"], TPC * (c - 1))
                dve.wait_ge(loaded[b], 16 * (c - b) + 32)
                dve.wait_ge(gathered[b], TPC * 16 * (c - b) + 2 * TPC * 16)
                for t in range(TPC):
                    wa = weight[:, 0, ds(c * TPC + t, 1)]
                    dve.scalar_tensor_tensor(tile_of(ya, c, t), tile_of(ya, c, t), wa, tile_of(h, c, t),
                                             ALU.mult, ALU.add).then_inc(s["m1"], 1)
                for t in range(TPC):
                    wb = weight[:, 1, ds(c * TPC + t, 1)]
                    dve.wait_ge(s["m1"], TPC * c + (t + 1))
                    dve.scalar_tensor_tensor(a[:, b, t], tile_of(yb, c, t), wb, tile_of(ya, c, t), ALU.mult, ALU.add)\
                       .then_inc(s["m2"], 1)

            def moments(c, b):
                for t in range(TPC):
                    dve.wait_ge(s["m2"], TPC * c + (t + 1))
                    dve.bn_stats(st[:, 0, t], a[:, b, t]).then_inc(s["sta"], 1)
                pause(dve, s["sta"], TPC * c + TPC, s["passed"])
                for t in range(TPC):
                    dve.bn_aggr(mv[:, 0, t], st[:, 0, t]).then_inc(s["mva"], 1)
                dve.wait_ge(s["mva"], TPC * c + TPC)
                dve.tensor_scalar(sm[:, 0], mv[:, 0, :, 1], LN_EPS, None, ALU.add).then_inc(s["a1"], 1)

            def norm1(c, b):
                dve.wait_ge(s["sd1"], c + 1)
                dve.reciprocal(sm[:, 2], sm[:, 1]).then_inc(s["a2"], 1)
                dve.wait_ge(s["a2"], 2 * c + 1)
                dve.scalar_tensor_tensor(sm[:, 7], mv[:, 0, :, 0], -1.0, sm[:, 2], ALU.mult, ALU.mult)\
                   .then_inc(s["a2"], 1)

            def affine(c, b):
                for j in range(2):
                    half = slice(2 * j, 2 * j + 2)
                    dve.wait_ge(s["na"], TPC * c + 2 * (j + 1))
                    dve.tensor_tensor(g[:, half], na[:, half], rows[:, 0].unsqueeze(1).broadcast_to([P, 2, D]),
                                      ALU.mult).then_inc(s["fg"], 1)
                ge(dve, s["r"], TPC * (c - 1))
                for j in range(2):
                    half = slice(2 * j, 2 * j + 2)
                    dve.wait_ge(s["fg"], 2 * c + (j + 1))
                    dve.tensor_tensor(f[:, b, half], g[:, half], rows[:, 1].unsqueeze(1).broadcast_to([P, 2, D]),
                                      ALU.add).then_inc(s["fb"], 1)
                for t in range(TPC):
                    if t % 2 == 0:
                        dve.wait_ge(s["fb"], 2 * c + (t // 2 + 1))
                    dve.bn_stats(st[:, 1, t], f[:, b, t]).then_inc(s["stf"], 1)
                pause(dve, s["stf"], TPC * c + TPC, s["passed"])
                for t in range(TPC):
                    dve.bn_aggr(mv[:, 1, t], st[:, 1, t]).then_inc(s["mvf"], 1)
                dve.wait_ge(s["mvf"], TPC * c + TPC)
                dve.tensor_scalar(sm[:, 3], mv[:, 1, :, 1], LN_EPS, None, ALU.add).then_inc(s["a3"], 1)

            def norm2(c, b):
                dve.wait_ge(s["sd2"], c + 1)
                dve.reciprocal(sm[:, 5], sm[:, 4]).then_inc(s["a4"], 1)
                dve.wait_ge(s["a4"], 2 * c + 1)
                dve.scalar_tensor_tensor(sm[:, 6], mv[:, 1, :, 0], -1.0, sm[:, 5], ALU.mult, ALU.mult)\
                   .then_inc(s["a4"], 1)

            chunks(dve.Fori, (norm1, 0), (gather, 1), (affine, 0), (moments, 1), (norm2, 0))

        body.close()
        m.clear()


def block_stack_kernel(nc, x, gate_w, gate_b, cand_w, cand_b, log_decay, out_wT, out_b, norm_w,
                       w_qkv, w_o, g1, b1, wg, w1, bb1, w2, bb2, g2, b2, out):
    def dram(name, shape, dt=F32):
        return nc.dram_tensor(name, shape, dt, kind="Internal").ap()

    x1_d, u2_d, h_d = (dram(n, [S, D]) for n in ("x1_d", "u2_d", "h_d"))
    qk_d = dram("qk_d", [3, 4, P, S], BF16)
    v_d = dram("v_d", [GROUPS, P, TILES, GROUP, HD + 1])
    oT_d = dram("oT_d", [HD + 1, HEADS, S])
    rz_d = dram("rz_d", [HEADS, S])
    places_d = dram("places_d", [TILE_SLOTS * PLACES, D])
    ys_d = dram("ys_d", [TILE_SLOTS * PLACES, D])
    with ExitStack() as ctx:
        m = Memory(nc, ctx, "k")
        ident = m.sb("ident", [P, P])
        place = m.sb("place", [P, 2, TILES], U32)
        weight = m.sb("weight", [P, 2, TILES])
        expert_of = m.sb("expert_of", [P, TILE_SLOTS], I32)
        front_phase(nc, ident, x, gate_w, gate_b, cand_w, cand_b, log_decay, out_wT, out_b, norm_w, w_qkv,
                    x1_d, u2_d, qk_d, v_d)
        attention_phase(nc, qk_d, v_d, oT_d, places_d)
        with nc.sbuf_tensor("stage", [P, 2, 2, DH * F], F32) as stage:
            route_phase(nc, ident, oT_d, rz_d, u2_d, w_o, g1, b1, wg, w1, w2, h_d, places_d, place, weight,
                        expert_of, stage)
            expert_phase(nc, ident, stage, places_d, w1, bb1, w2, bb2, expert_of, ys_d)
        final_phase(nc, ys_d, h_d, x1_d, place, weight, g2, b2, out)


def kernel(**inputs):
    import numpy as np
    from concourse import bacc
    from concourse.bass_utils import run_bass_kernel_spmd

    a = {n.split("_", 2)[2]: np.asarray(v) for n, v in inputs.items()}

    def per_partition(v):
        return v.reshape(DH, P).T

    arrays = {
        "x": a["x"].reshape(S, D),
        "gate_w": a["gate_w"], "gate_b": per_partition(a["gate_b"]),
        "cand_w": a["cand_w"], "cand_b": per_partition(a["cand_b"]),
        "log_decay": per_partition(a["log_decay"]),
        "out_wT": a["out_w"].T, "out_b": a["out_b"], "norm_w": a["norm_w"], "w_qkv": a["w_qkv"],
        "w_o": a["w_o"].reshape(HEADS, HD, D).transpose(1, 0, 2).reshape(D, D),
        "g1": a["g1"], "b1": a["b1"], "wg": a["wg"], "w1": a["w1"],
        "bb1": a["bb1"].reshape(EXPERTS, FB, P).transpose(2, 0, 1).reshape(P, EXPERTS * FB),
        "w2": a["w2"], "bb2": a["bb2"], "g2": a["g2"], "b2": a["b2"],
    }
    nc = bacc.Bacc("TRN2", target_bir_lowering=False, num_devices=1)
    sent, args = {}, []
    for name, v in arrays.items():
        v = np.ascontiguousarray(v)
        sent[f"in_{name}"] = v
        args.append(nc.dram_tensor(f"in_{name}", v.shape, mybir.dt.from_np(v.dtype), kind="ExternalInput").ap())
    args.append(nc.dram_tensor("out", (S, D), F32, kind="ExternalOutput").ap())
    block_stack_kernel(nc, *args)
    r = run_bass_kernel_spmd(nc, [sent], core_ids=[0])
    return r.results[0]["out"].reshape(1, S, D)
```
